# Optimizing a Trainium2 kernel written in Bass

```python
import numpy as np
import jax
import jax.numpy as jnp

def _softmax(x, axis=-1):
    return jax.nn.softmax(x, axis=axis)

def _gelu(x):
    return jax.nn.gelu(x, approximate=True)

def _silu(x):
    return jax.nn.silu(x)

def _sigmoid(x):
    return jax.nn.sigmoid(x)

def _layernorm(x, axis=-1, eps=1e-05):
    m = jnp.mean(x, axis=axis, keepdims=True)
    v = jnp.var(x, axis=axis, keepdims=True)
    return (x - m) / jnp.sqrt(v + eps)

def _scatter_add(tgt, idx, src, axis=0):
    return tgt.at[idx].add(src)

def _segment_sum(src, seg, n):
    return jax.ops.segment_sum(src, seg, n)
kernel_name = 'mk_macaron_d1_jaxref_r8_dc1da6'

def setup_inputs(seed: int=0):
    np.random.seed(seed)
    _w = jnp.asarray

    def _L0_attn_setup():
        import jax, jax.numpy as jnp
        import numpy as np
        HEAD_DIM = 64
        N_HEADS = 16
        BASE = 10000.0
        SCALES = (1.0, 4.0, 16.0)

        def _avg_cos_sin(T, head_dim, base, scales):
            pos = jnp.arange(T, dtype=jnp.float32)
            i = jnp.arange(head_dim // 2, dtype=jnp.float32)
            coss, sins = ([], [])
            for s in scales:
                freqs = 1.0 / (base * s) ** (2.0 * i / head_dim)
                ang = pos[:, None] * freqs[None, :]
                coss.append(jnp.cos(ang))
                sins.append(jnp.sin(ang))
            return (jnp.mean(jnp.stack(coss), 0), jnp.mean(jnp.stack(sins), 0))

        def _rope(x, cos, sin):
            xe = x[..., 0::2]
            xo = x[..., 1::2]
            re = xe * cos - xo * sin
            ro = xe * sin + xo * cos
            return jnp.stack([re, ro], axis=-1).reshape(x.shape)
        key = jax.random.key(seed)
        ks = jax.random.split(key, 5)
        B, T, D = (2, 256, 128)
        s = 1.0 / np.sqrt(D)
        return {'x': jax.random.normal(ks[0], (B, T, D), dtype=jnp.float32), 'Wq': jax.random.normal(ks[1], (D, N_HEADS * HEAD_DIM), dtype=jnp.float32) * s, 'Wk': jax.random.normal(ks[2], (D, N_HEADS * HEAD_DIM), dtype=jnp.float32) * s, 'Wv': jax.random.normal(ks[3], (D, N_HEADS * HEAD_DIM), dtype=jnp.float32) * s, 'Wo': jax.random.normal(ks[4], (N_HEADS * HEAD_DIM, D), dtype=jnp.float32) * s}
    _L0_attn_in = _L0_attn_setup()

    def _L0_ffn_setup():
        import jax, jax.numpy as jnp
        import numpy as np
        H, E, DFF = (128, 8, 512)
        key = jax.random.key(seed)
        ks = jax.random.split(key, 7)
        s = lambda *shape: 1.0 / np.sqrt(shape[-2] if len(shape) > 1 else shape[-1])
        x = jax.random.normal(ks[0], (2, 256, H), dtype=jnp.float32)
        Wr = jax.random.normal(ks[1], (H, E), dtype=jnp.float32) * (1.0 / np.sqrt(H))
        br = jnp.zeros((E,), dtype=jnp.float32)
        W1 = jax.random.normal(ks[2], (E, H, DFF), dtype=jnp.float32) * (1.0 / np.sqrt(H))
        b1 = jnp.zeros((E, DFF), dtype=jnp.float32)
        W2 = jax.random.normal(ks[3], (E, DFF, H), dtype=jnp.float32) * (1.0 / np.sqrt(DFF))
        b2 = jnp.zeros((E, H), dtype=jnp.float32)
        return {'x': x, 'Wr': Wr, 'br': br, 'W1': W1, 'b1': b1, 'W2': W2, 'b2': b2}
    _L0_ffn_in = _L0_ffn_setup()
    _d = {'L0_attn_x': _L0_attn_in['x'], 'L0_attn_Wq': _L0_attn_in['Wq'], 'L0_attn_Wk': _L0_attn_in['Wk'], 'L0_attn_Wv': _L0_attn_in['Wv'], 'L0_attn_Wo': _L0_attn_in['Wo'], 'L0_ffn_Wr': _L0_ffn_in['Wr'], 'L0_ffn_br': _L0_ffn_in['br'], 'L0_ffn_W1': _L0_ffn_in['W1'], 'L0_ffn_b1': _L0_ffn_in['b1'], 'L0_ffn_W2': _L0_ffn_in['W2'], 'L0_ffn_b2': _L0_ffn_in['b2']}
    _x0 = _d['L0_attn_x']
    _d['L0_attn_x'] = jax.random.normal(jax.random.fold_in(jax.random.key(seed), 1), (16, 256, 128), dtype=_x0.dtype)
    del _x0
    return _d

def reference(L0_attn_x, L0_attn_Wq, L0_attn_Wk, L0_attn_Wv, L0_attn_Wo, L0_ffn_Wr, L0_ffn_br, L0_ffn_W1, L0_ffn_b1, L0_ffn_W2, L0_ffn_b2):

    def _L0_attn_ref(x, Wq, Wk, Wv, Wo):
        import jax, jax.numpy as jnp
        import numpy as np
        HEAD_DIM = 64
        N_HEADS = 16
        BASE = 10000.0
        SCALES = (1.0, 4.0, 16.0)

        def _avg_cos_sin(T, head_dim, base, scales):
            pos = jnp.arange(T, dtype=jnp.float32)
            i = jnp.arange(head_dim // 2, dtype=jnp.float32)
            coss, sins = ([], [])
            for s in scales:
                freqs = 1.0 / (base * s) ** (2.0 * i / head_dim)
                ang = pos[:, None] * freqs[None, :]
                coss.append(jnp.cos(ang))
                sins.append(jnp.sin(ang))
            return (jnp.mean(jnp.stack(coss), 0), jnp.mean(jnp.stack(sins), 0))

        def _rope(x, cos, sin):
            xe = x[..., 0::2]
            xo = x[..., 1::2]
            re = xe * cos - xo * sin
            ro = xe * sin + xo * cos
            return jnp.stack([re, ro], axis=-1).reshape(x.shape)
        B, T, D = x.shape
        H, hd = (N_HEADS, HEAD_DIM)
        q = (x @ Wq).reshape(B, T, H, hd).transpose(0, 2, 1, 3)
        k = (x @ Wk).reshape(B, T, H, hd).transpose(0, 2, 1, 3)
        v = (x @ Wv).reshape(B, T, H, hd).transpose(0, 2, 1, 3)
        cos, sin = _avg_cos_sin(T, hd, BASE, SCALES)
        q = _rope(q, cos, sin)
        k = _rope(k, cos, sin)
        scale = 1.0 / np.sqrt(hd).astype(np.float32)
        attn = jax.nn.softmax(jnp.einsum('bhqd,bhkd->bhqk', q, k) * scale, axis=-1)
        out = jnp.einsum('bhqk,bhkd->bhqd', attn, v)
        out = out.transpose(0, 2, 1, 3).reshape(B, T, H * hd)
        return out @ Wo

    def _L0_ffn_ref(x, Wr, br, W1, b1, W2, b2):
        import jax, jax.numpy as jnp
        import numpy as np
        H, E, DFF = (128, 8, 512)
        B, S, Hd = x.shape
        n_exp = W1.shape[0]
        xt = x.reshape(-1, Hd)
        logits = xt @ Wr + br
        probs = jax.nn.softmax(logits, axis=-1)
        gate = jnp.max(probs, axis=-1)
        idx = jnp.argmax(probs, axis=-1)
        h1 = jnp.maximum(jnp.einsum('th,ehf->etf', xt, W1) + b1[:, None, :], 0.0)
        ye = jnp.einsum('etf,efh->eth', h1, W2) + b2[:, None, :]
        onehot = jax.nn.one_hot(idx, n_exp, dtype=xt.dtype)
        y = jnp.einsum('te,eth->th', onehot, ye) * gate[:, None]
        return y.reshape(B, S, Hd)
    x = L0_attn_x
    x = x + 0.5 * _L0_ffn_ref(_layernorm(x, axis=-1), L0_ffn_Wr, L0_ffn_br, L0_ffn_W1, L0_ffn_b1, L0_ffn_W2, L0_ffn_b2)
    x = x + _L0_attn_ref(_layernorm(x, axis=-1), L0_attn_Wq, L0_attn_Wk, L0_attn_Wv, L0_attn_Wo)
    x = x + 0.5 * _L0_ffn_ref(_layernorm(x, axis=-1), L0_ffn_Wr, L0_ffn_br, L0_ffn_W1, L0_ffn_b1, L0_ffn_W2, L0_ffn_b2)
    return x

_drawn_inputs = setup_inputs


def setup_inputs(seed=0):
    import zlib

    import numpy as np

    out = dict(_drawn_inputs(seed))
    spreads = {'L0_ffn_br': (0.0, 0.1), 'L0_ffn_b1': (0.0, 0.271), 'L0_ffn_b2': (0.0, 0.1)}
    factors = {}
    for name, (base, spread) in spreads.items():
        noise = np.random.default_rng([zlib.crc32(name.encode()), seed]).standard_normal(out[name].shape)
        drawn = base * np.exp(spread * noise) if base else spread * noise
        out[name] = jnp.asarray(drawn.astype(out[name].dtype))
    for name, factor in factors.items():
        out[name] = (out[name] * factor).astype(out[name].dtype)
    return out
```

```python
from contextlib import ExitStack

import concourse.bass as bass
from concourse import mybir

F32 = mybir.dt.float32
F32R = mybir.dt.float32r
I32 = mybir.dt.int32
U32 = mybir.dt.uint32
ALU = mybir.AluOpType
ACT = mybir.ActivationFunctionType
AX = mybir.AxisListType

P = 128
BATCH, SEQ, D = 16, 256, 128
HEADS, HEAD = 16, 64
EXPERTS, DFF = 8, 512
TILES = BATCH * SEQ // P
QT = SEQ // P
NG = TILES + EXPERTS
FC = DFF // P
HALF = HEADS // 2
PAIRS = HALF // 2
EPS = 1e-5
ROW = 4
RING = 4

C_ID, C_LOW, C_ONE = 0, P, 2 * P
C_ROPE = 3 * P
C_DESC = C_ROPE + 4 * QT * HEAD
C_THR = C_DESC + EXPERTS
C_TIX = C_THR + TILES
C_ALL = C_TIX + NG


def constants():
    import numpy as np

    f = np.float32
    c = np.zeros((P, C_ALL), f)
    c[:, C_ID:C_ID + P] = np.eye(P, dtype=f)
    c[:, C_LOW:C_LOW + P] = np.triu(np.ones((P, P), f), 1)
    c[:, C_ONE:C_ONE + P] = 1
    pos = np.arange(SEQ, dtype=f)
    i = np.arange(HEAD // 2, dtype=f)
    cos, sin = [], []
    for s in (1.0, 4.0, 16.0):
        freq = f(1.0) / np.power(f(10000.0 * s), f(2.0) * i / f(HEAD), dtype=f)
        ang = pos[:, None] * freq[None, :]
        cos.append(np.cos(ang))
        sin.append(np.sin(ang))
    cos = np.mean(np.stack(cos), 0, dtype=f)
    sin = np.mean(np.stack(sin), 0, dtype=f)
    scale = f(HEAD) ** f(-0.5)
    for n, (a, b) in enumerate(((cos, cos), (sin, -sin))):
        t = np.concatenate([a, b], 1).reshape(QT, P, HEAD).transpose(1, 0, 2).reshape(P, QT * HEAD)
        at = C_ROPE + n * QT * HEAD
        c[:, at:at + QT * HEAD] = t * scale
        c[:, at + 2 * QT * HEAD:at + 3 * QT * HEAD] = t
    c[:, C_DESC:C_DESC + EXPERTS] = np.arange(EXPERTS, 0, -1)
    c[:, C_THR:C_THR + TILES] = P * np.arange(TILES)
    c[:, C_TIX:C_TIX + NG] = np.arange(NG)
    return c


def macaron_kernel(nc, x, wq, wk, wv, wo, wr, br, w1, b1, w2, b2, consts, out):
    x_t = x.rearrange("b (n p) d -> p (b n) d", p=P)
    out_t = out.rearrange("b (n p) d -> p (b n) d", p=P)
    grouped_x = nc.dram_tensor("grouped_x", [NG * P, D], F32).ap()
    grouped_y = nc.dram_tensor("grouped_y", [NG * P, D], F32).ap()

    with ExitStack() as ctx:
        def sb(name, shape, dt=F32):
            return ctx.enter_context(nc.sbuf_tensor(name, shape, dt))

        def sem(name):
            return ctx.enter_context(nc.semaphore(name))

        bank = [ctx.enter_context(nc.psum_tensor(f"bank{n}", [P, 512], F32)) for n in range(8)]

        con = sb("con", [P, C_ALL])
        X = sb("X", [P, TILES, D])
        XN = sb("XN", [P, TILES, D])
        W1 = sb("W1", [P, EXPERTS * DFF])
        W2 = sb("W2", [P, EXPERTS * FC * D])
        b1_rows = sb("b1_rows", [EXPERTS * FC, P])
        b1_col = sb("b1_col", [P, EXPERTS * FC])
        b2_all = sb("b2_all", [P, EXPERTS * D])
        Wr = sb("Wr", [P, EXPERTS])
        br_all = sb("br_all", [P, EXPERTS])
        zero = sb("zero", [P, D])
        ones = sb("ones", [P, TILES * EXPERTS])
        w_raw = sb("w_raw", [P, 6, 512])
        w_hi = sb("w_hi", [P, 6, 512], F32R)
        w_lo = sb("w_lo", [P, 6, 512], F32R)
        Wo = sb("Wo", [P, HEADS // 2, D])
        stats = sb("stats", [P, TILES, 6])
        mv = sb("mv", [P, TILES, 2])
        ln = sb("ln", [P, 6, TILES])
        rstd = ln[:, 5, :]
        XNT = sb("XNT", [P, 2, ROW * P])
        R = sb("R", [P, 8, TILES * EXPERTS])
        small = sb("small", [P, 12, TILES])
        first_le = sb("first_le", [P, NG, EXPERTS - 1])
        expert_f = sb("expert_f", [P, NG])
        expert_of = sb("expert_of", [P, NG], I32)
        place = sb("place", [P, TILES], U32)
        half_gate = sb("half_gate", [P, TILES])
        XG = sb("XG", [P, RING, D])
        XT = sb("XT", [P, 2, P])
        shared = sb("shared", [P, 4 * DFF])
        Hs = shared[:, 0:2 * DFF].rearrange("p (r f) -> p r f", r=2)
        HT = shared[:, 2 * DFF:4 * DFF].rearrange("p (r c t) -> p r c t", r=2, c=FC)
        Y = sb("Y", [P, RING, D])
        xn = sb("xn", [P, QT, D])
        xT_hi = sb("xT_hi", [P, SEQ], F32R)
        xT_lo = sb("xT_lo", [P, SEQ], F32R)
        rot_u = sb("rot_u", [P, 2, 512])
        rot_w = sb("rot_w", [P, 2, 512])
        rot = XN[:, 0:2 * QT * 4, :].rearrange("p (k t c) d -> p k t (c d)", k=2, t=QT)
        qk_hi = sb("qk_hi", [P, 2, PAIRS, 2, SEQ], F32R)
        qk_lo = sb("qk_lo", [P, 2, PAIRS, 2, SEQ], F32R)
        V = sb("V", [P, 2, QT, 512])
        negmax = sb("negmax", [P, 2, QT])
        total = sb("total", [P, 2, QT])
        recip = sb("recip", [P, 2, QT])
        E = sb("E", [P, 4, QT, SEQ])
        ET = sb("ET", [P, 2, QT * SEQ])
        OT = shared[:, :].rearrange("p (j s) -> p j s", j=HEADS // 2)

        ident = con[:, C_ID:C_ID + P]
        lower = con[:, C_LOW:C_LOW + P]
        ones_sq = con[:, C_ONE:C_ONE + P]

        def table(kind, which, tt):
            at = C_ROPE + ((2 * kind + which) * QT + tt) * HEAD
            return con[:, at:at + HEAD]

        x_in = [sem(f"x_in{n}") for n in range(4)]
        con_in = sem("con_in")
        small_in = sem("small_in")
        ffn_w_in = sem("ffn_w_in")
        attn_w_in = sem("attn_w_in")
        const_set = sem("const_set")
        zero_fill = sem("zero_fill")
        w_hi_set = sem("w_hi_set")
        w_lo_set = sem("w_lo_set")
        b1_turned = sem("b1_turned")
        b1_set = sem("b1_set")
        dve_step = sem("dve_step")
        out_done = sem("out_done")
        steps = [0]

        def link(eng, ins):
            ins.then_inc(dve_step, 1)
            steps[0] += 1
            eng.wait_ge(dve_step, steps[0])

        class Sems:
            pass

        def ffn_sems(n):
            s = Sems()
            s.var_ready = sem(f"f{n}_var_ready")
            s.sqrt_ready = sem(f"f{n}_sqrt_ready")
            s.normed = sem(f"f{n}_normed")
            s.turned = sem(f"f{n}_turned")
            s.turned_out = sem(f"f{n}_turned_out")
            s.logits = sem(f"f{n}_logits")
            s.shifted = sem(f"f{n}_shifted")
            s.exped = sem(f"f{n}_exped")
            s.onehot = sem(f"f{n}_onehot")
            s.ranked = sem(f"f{n}_ranked")
            s.routed = sem(f"f{n}_routed")
            s.scattered = sem(f"f{n}_scattered")
            s.xg_in = [sem(f"f{n}_xg_in{r}") for r in range(RING)]
            s.xt_mm = sem(f"f{n}_xt_mm")
            s.xt_out = sem(f"f{n}_xt_out")
            s.h_mm = sem(f"f{n}_h_mm")
            s.h_out = sem(f"f{n}_h_out")
            s.ht_mm = sem(f"f{n}_ht_mm")
            s.ht_out = sem(f"f{n}_ht_out")
            s.y_mm = sem(f"f{n}_y_mm")
            s.y_out = sem(f"f{n}_y_out")
            s.y_stored = [sem(f"f{n}_y_stored{r}") for r in range(RING)]
            s.gathered = [sem(f"f{n}_gathered{r}") for r in range(TILES // ROW)]
            s.added = sem(f"f{n}_added")
            return s

        ffn = [ffn_sems(0), ffn_sems(1)]

        ln2_var = sem("ln2_var")
        ln2_sqrt = sem("ln2_sqrt")
        xn_set = sem("xn_set")
        xT_mm = sem("xT_mm")
        xT_hi_set = sem("xT_hi_set")
        xT_lo_set = sem("xT_lo_set")
        proj_mm = sem("proj_mm")
        rope_w = sem("rope_w")
        rot_set = sem("rot_set")
        v_set = sem("v_set")
        turn_mm = sem("turn_mm")
        qk_hi_set = sem("qk_hi_set")
        qk_lo_set = sem("qk_lo_set")
        score_mm = sem("score_mm")
        max_set = sem("max_set")
        exp_set = sem("exp_set")
        recip_set = sem("recip_set")
        prob_set = sem("prob_set")
        et_mm = sem("et_mm")
        et_set = sem("et_set")
        pv_mm = sem("pv_mm")
        ot_set = sem("ot_set")
        wo_mm = sem("wo_mm")
        wo_added = sem("wo_added")
        attn_done = wo_added

        block = ctx.enter_context(nc.Block())

        def ffn_load_store(sp, s):
            def load(j, r, free):
                if free is not None:
                    sp.wait_ge(s.xt_mm, free)
                sp.dma_start(XG[:, r, :], grouped_x[bass.ds(j * P, P), :]).then_inc(s.xg_in[r], 16)

            def store(j, r):
                sp.wait_ge(s.y_out, j + 1)
                sp.dma_start(grouped_y[bass.ds(j * P, P), :], Y[:, r, :]).then_inc(s.y_stored[r], 16)

            sp.wait_ge(s.scattered, 16 * TILES)
            for j in range(2 * RING):
                load(j, j % RING, j - RING + 1 if j >= RING else None)
            with sp.Fori(2, NG // RING) as q:
                for r in range(RING):
                    load(q * RING + r, r, q * RING + (r - RING + 1))
                    store(q * RING + (r - 2 * RING), r)
            for j in range(NG - 2 * RING, NG):
                store(j, j % RING)

        def ffn_tensor(pe, s, n):
            for g in range(TILES // ROW):
                pe.wait_ge(s.normed, ROW * (g + 1))
                if g >= 2:
                    pe.wait_ge(s.turned_out, g - 1)
                for k in range(ROW):
                    t = g * ROW + k
                    mm = pe.transpose(bank[g % 2][:, k * P:(k + 1) * P], XN[:, t, :], ident)
                mm.then_inc(s.turned, 1)
                if g == 0 and n == 0:
                    pe.wait_ge(small_in, 16 * 4)
                    pe.transpose(bank[4][:, 0:EXPERTS * FC], b1_rows[:, :],
                                 con[0:EXPERTS * FC, C_ID:C_ID + EXPERTS * FC]).then_inc(b1_turned, 1)
                if g >= 1:
                    logits(pe, s, g - 1)
            logits(pe, s, TILES // ROW - 1)
            pe.wait_ge(s.onehot, 1)
            onehot = R[:, 3, :]
            pe.matmul(bank[3][:, 0:TILES * EXPERTS], lower, onehot, start=True, stop=True)
            pe.matmul(bank[4][:, 0:TILES * EXPERTS], ones_sq, onehot, start=True, stop=True).then_inc(s.ranked, 1)

            def turn_x(j, r, p):
                pe.wait_ge(s.xg_in[r], (j // RING + 1 if isinstance(j, int) else j) * 16)
                pe.transpose(bank[0][:, 0:P], XG[:, r, :], ident).then_inc(s.xt_mm, 1)

            def slot(j, r, first=False, tx=True, w1=True, th=True, w2=True, q=None):
                p = r % 2
                if w1:
                    e = pe.value_load(expert_of[0:1, bass.ds(j, 1)], min_val=0, max_val=EXPERTS - 1)
                    pe.wait_ge(s.xt_out, j + 1)
                    if not first:
                        pe.wait_ge(s.h_out, j - 1)
                    pe.matmul(bank[1 + p][:, :], XT[:, p, :], W1[:, bass.ds(e * DFF, DFF)],
                              start=True, stop=True).then_inc(s.h_mm, 1)
                if w2:
                    e2 = pe.value_load(expert_of[0:1, bass.ds(j - 2, 1)], min_val=0, max_val=EXPERTS - 1)
                    pe.wait_ge(s.ht_out, j - 1)
                    if not (isinstance(j, int) and j < 4):
                        pe.wait_ge(s.y_out, j - 3)
                    for c in range(FC):
                        mm = pe.matmul(bank[5 + p][:, 0:D], HT[:, p, c, :],
                                       W2[:, bass.ds(e2 * (FC * D) + c * D, D)],
                                       start=(c == 0), stop=(c == FC - 1))
                    mm.then_inc(s.y_mm, 1)
                if th:
                    pe.wait_ge(s.h_out, j)
                    if not (isinstance(j, int) and j < 3):
                        pe.wait_ge(s.ht_out, j - 2)
                    for c in range(FC):
                        mm = pe.transpose(bank[3 + (1 - p)][:, c * P:(c + 1) * P],
                                          Hs[:, 1 - p, c * P:(c + 1) * P], ident)
                    mm.then_inc(s.ht_mm, 1)
                if tx:
                    nr = (r + 1) % RING
                    pe.wait_ge(s.xg_in[nr], (q + (1 if nr else 2)) * 16)
                    pe.wait_ge(s.xt_out, j + 1)
                    pe.transpose(bank[0][:, 0:P], XG[:, nr, :], ident).then_inc(s.xt_mm, 1)

            pe.wait_ge(s.routed, 1)
            if n == 0:
                pe.wait_ge(ffn_w_in, 32)
            pe.wait_ge(s.xg_in[0], 16)
            pe.transpose(bank[0][:, 0:P], XG[:, 0, :], ident).then_inc(s.xt_mm, 1)
            for j in range(RING):
                slot(j, j, first=j < 2, th=j >= 1, w2=j >= 2, q=0)
            with pe.Fori(1, NG // RING - 1) as q:
                for r in range(RING):
                    slot(q * RING + r, r, q=q)
            for j in range(NG - RING, NG):
                slot(j, j % RING, tx=j < NG - 1, q=NG // RING - 1)
            slot(NG, 0, w1=False, tx=False)
            slot(NG + 1, 1, w1=False, th=False, tx=False)

        def logits(pe, s, g):
            pe.wait_ge(s.turned_out, g + 1)
            for k in range(ROW):
                t = g * ROW + k
                mm = pe.matmul(bank[2][:, t * EXPERTS:(t + 1) * EXPERTS], XNT[:, g % 2, k * P:(k + 1) * P],
                               Wr[:, :], start=True, stop=True)
            mm.then_inc(s.logits, 1)

        def ffn_scalar(act, s):
            act.wait_ge(s.var_ready, 1)
            act.activation(ln[:, 1, :], ln[:, 0, :], ACT.Sqrt).then_inc(s.sqrt_ready, 1)
            for g in range(TILES // ROW):
                act.wait_ge(s.turned, g + 1)
                if g >= 2:
                    act.wait_ge(s.logits, g - 1)
                act.activation(XNT[:, g % 2, :], bank[g % 2][:, :], ACT.Copy).then_inc(s.turned_out, 1)
            act.wait_ge(s.shifted, 1)
            act.activation(R[:, 4, :], R[:, 1, :], ACT.Exp).then_inc(s.exped, 1)

            def slot(j, p, h=True, xt=True, first=False):
                if h:
                    act.wait_ge(s.h_mm, j)
                    if not (isinstance(j, int) and j < 3):
                        act.wait_ge(s.ht_mm, j - 2)
                    act.activation(Hs[:, 1 - p, :], bank[1 + (1 - p)][:, :], ACT.Copy).then_inc(s.h_out, 1)
                if xt:
                    act.wait_ge(s.xt_mm, j + 1)
                    if not first:
                        act.wait_ge(s.h_mm, j - 1)
                    act.activation(XT[:, p, :], bank[0][:, 0:P], ACT.Copy).then_inc(s.xt_out, 1)

            for j in range(2):
                slot(j, j, h=j >= 1, first=True)
            with act.Fori(1, NG // 2) as q:
                for p in range(2):
                    slot(q * 2 + p, p)
            slot(NG, 0, xt=False)

        def norm_stats(dve, s_var, s_sqrt):
            link(dve, dve.tensor_scalar(ln[:, 0, :], mv[:, :, 1], EPS, None, ALU.add))
            dve.drain().then_inc(s_var, 1)
            dve.wait_ge(s_sqrt, 1)
            link(dve, dve.reciprocal(ln[:, 2, :], ln[:, 1, :]))
            link(dve, dve.tensor_tensor(ln[:, 3, :], ln[:, 0, :], ln[:, 2, :], ALU.mult))
            link(dve, dve.tensor_tensor(ln[:, 4, :], ln[:, 1, :], ln[:, 3, :], ALU.add))
            link(dve, dve.tensor_scalar(ln[:, 3, :], ln[:, 4, :], 0.5, None, ALU.mult))
            link(dve, dve.reciprocal(rstd, ln[:, 3, :]))

        def aggregate(dve):
            for t in range(TILES):
                ins = dve.bn_aggr(mv[:, t, :], stats[:, t, :])
            link(dve, ins)

        def ffn_vector(dve, s, n):
            if n == 0:
                for g in range(4):
                    dve.wait_ge(x_in[g], 16)
                    for t in range(8 * g, 8 * g + 8):
                        ins = dve.bn_stats(stats[:, t, :], X[:, t, :])
            else:
                for t in range(TILES):
                    ins = dve.bn_stats(stats[:, t, :], X[:, t, :])
            link(dve, ins)
            aggregate(dve)
            norm_stats(dve, s.var_ready, s.sqrt_ready)
            for t in range(TILES):
                dve.tensor_scalar(XN[:, t, :], X[:, t, :], mv[:, t, 0:1], rstd[:, t:t + 1],
                                  ALU.subtract, ALU.mult).then_inc(s.normed, 1)
            if n == 0:
                dve.wait_ge(b1_turned, 1)
                dve.tensor_copy(b1_col[:, :], bank[4][:, 0:EXPERTS * FC]).then_inc(b1_set, 1)
                dve.wait_ge(b1_set, 1)
                dve.wait_ge(con_in, 16)
                dve.wait_ge(small_in, 16 * 4)

            def te(ap):
                return ap.rearrange("p (t e) -> p t e", e=EXPERTS)

            def et(ap):
                return ap.rearrange("p (e t) -> p e t", t=TILES)

            def by_tile(v):
                return v.unsqueeze(2).to_broadcast([P, TILES, EXPERTS])

            full = [P, TILES, EXPERTS]
            desc = con[:, C_DESC:C_DESC + EXPERTS].unsqueeze(1).to_broadcast(full)
            lg, sh, cand, oh, ex, cnt, inc, exc = (R[:, k, :] for k in range(8))
            mx, cm, se = small[:, 0, :], small[:, 1, :], small[:, 2, :]
            n_of, n_tiles, upto, before, adj = (small[:, k, 0:EXPERTS] for k in range(3, 8))
            place_f = small[:, 8, :]
            dve.wait_ge(s.logits, TILES // ROW)
            link(dve, dve.tensor_tensor(te(lg), te(bank[2][:, 0:TILES * EXPERTS]),
                                        br_all[:, :].unsqueeze(1).to_broadcast(full), ALU.add))
            link(dve, dve.tensor_reduce(mx, te(lg), AX.X, ALU.max))
            dve.tensor_tensor(te(sh), te(lg), by_tile(mx), ALU.subtract).then_inc(s.shifted, 1)
            link(dve, dve.tensor_tensor(te(cand), te(lg), by_tile(mx), ALU.is_equal))
            link(dve, dve.tensor_tensor(te(cand), te(cand), desc, ALU.mult))
            link(dve, dve.tensor_reduce(cm, te(cand), AX.X, ALU.max))
            dve.tensor_tensor(te(oh), te(cand), by_tile(cm), ALU.is_equal).then_inc(s.onehot, 1)
            dve.wait_ge(s.exped, 1)
            link(dve, dve.tensor_reduce(se, te(ex), AX.X, ALU.add))
            link(dve, dve.reciprocal(small[:, 9, :], se))
            link(dve, dve.tensor_scalar(half_gate[:, :], small[:, 9, :], 0.5, None, ALU.mult))
            dve.wait_ge(s.ranked, 1)
            link(dve, dve.tensor_copy(et(cnt), te(bank[4][:, 0:TILES * EXPERTS]).rearrange("p t e -> p e t")))
            dve.wait_ge(const_set, 2)
            link(dve, dve.tensor_tensor_scan(inc, ones[:, :], cnt, 0.0, ALU.mult, ALU.add))
            link(dve, dve.tensor_tensor(exc, inc, cnt, ALU.subtract))
            link(dve, dve.tensor_reduce(n_of, et(cnt), AX.X, ALU.add))
            thr = con[:, C_THR:C_THR + TILES].unsqueeze(1).to_broadcast([P, EXPERTS, TILES])
            link(dve, dve.tensor_tensor(et(sh), n_of.unsqueeze(2).to_broadcast([P, EXPERTS, TILES]), thr, ALU.is_gt))
            link(dve, dve.tensor_reduce(n_tiles, et(sh), AX.X, ALU.add))
            link(dve, dve.tensor_tensor_scan(upto, ones[:, 0:EXPERTS], n_tiles, 0.0, ALU.mult, ALU.add))
            link(dve, dve.tensor_tensor(before, upto, n_tiles, ALU.subtract))
            link(dve, dve.scalar_tensor_tensor(out=adj, in0=before, scalar=float(P), in1=et(exc)[:, :, 0],
                                               op0=ALU.mult, op1=ALU.subtract))
            link(dve, dve.tensor_tensor(et(inc), et(exc), adj.unsqueeze(2).to_broadcast([P, EXPERTS, TILES]), ALU.add))
            link(dve, dve.tensor_tensor(te(sh), te(bank[3][:, 0:TILES * EXPERTS]),
                                        et(inc).rearrange("p e t -> p t e"), ALU.add))
            link(dve, dve.tensor_tensor(sh, sh, oh, ALU.mult))
            link(dve, dve.tensor_reduce(place_f, te(sh), AX.X, ALU.add))
            link(dve, dve.tensor_copy(place[:, :], place_f))
            le = [P, NG, EXPERTS - 1]
            link(dve, dve.tensor_tensor(first_le[:, :, :], upto[:, 0:EXPERTS - 1].unsqueeze(1).to_broadcast(le),
                                        con[:, C_TIX:C_TIX + NG].unsqueeze(2).to_broadcast(le), ALU.is_le))
            link(dve, dve.tensor_reduce(expert_f[:, :], first_le[:, :, :], AX.X, ALU.add))
            dve.tensor_copy(expert_of[:, :], expert_f[:, :]).then_inc(s.routed, 1)
            dve.wait_ge(s.routed, 1)

            def relu(j, p):
                e = dve.value_load(expert_of[0:1, bass.ds(j, 1)], min_val=0, max_val=EXPERTS - 1)
                dve.wait_ge(s.ht_mm, j + 1)
                if not (isinstance(j, int) and j < 2):
                    dve.wait_ge(s.y_mm, j - 1)
                for c in range(FC):
                    ins = dve.tensor_scalar(HT[:, p, c, :], bank[3 + p][:, c * P:(c + 1) * P],
                                            b1_col[:, bass.ds(e * FC + c, 1)], 0.0, ALU.add, ALU.max)
                ins.then_inc(s.ht_out, 1)

            def add_b2(j, r, q):
                e = dve.value_load(expert_of[0:1, bass.ds(j, 1)], min_val=0, max_val=EXPERTS - 1)
                dve.wait_ge(s.y_mm, j + 1)
                if q is not None:
                    dve.wait_ge(s.y_stored[r], q * 16)
                dve.tensor_tensor(Y[:, r, :], bank[5 + r % 2][:, 0:D], b2_all[:, bass.ds(e * D, D)],
                                  ALU.add).then_inc(s.y_out, 1)

            for j in range(RING):
                relu(j, j % 2)
                if j >= 1:
                    add_b2(j - 1, j - 1, None)
            with dve.Fori(1, NG // RING) as q:
                for r in range(RING):
                    relu(q * RING + r, r % 2)
                    if r == 0:
                        add_b2_first(dve, s, q, add_b2)
                    else:
                        add_b2(q * RING + (r - 1), r - 1, q)
            add_b2(NG - 1, RING - 1, NG // RING - 1)

            for g in range(TILES // ROW):
                dve.wait_ge(s.gathered[g], 16 * ROW)
                for t in range(g * ROW, (g + 1) * ROW):
                    ins = dve.scalar_tensor_tensor(out=X[:, t, :], in0=XN[:, t, :], scalar=half_gate[:, t:t + 1],
                                                   in1=X[:, t, :], op0=ALU.mult, op1=ALU.add)
                ins.then_inc(s.added, 1)

        def add_b2_first(dve, s, q, add_b2):
            j = q * RING - 1
            e = dve.value_load(expert_of[0:1, bass.ds(j, 1)], min_val=0, max_val=EXPERTS - 1)
            dve.wait_ge(s.y_mm, j + 1)
            dve.wait_ge(s.y_stored[RING - 1], (q - 1) * 16)
            dve.tensor_tensor(Y[:, RING - 1, :], bank[5 + (RING - 1) % 2][:, 0:D], b2_all[:, bass.ds(e * D, D)],
                              ALU.add).then_inc(s.y_out, 1)

        def ffn_gpsimd(pool, s, n):
            pool.wait_ge(s.routed, 1)
            if n == 0:
                pool.wait_ge(zero_fill, 16)
            for t in range(TILES):
                pool.indirect_dma_start(out=grouped_x, out_offset=bass.IndirectOffsetOnAxis(ap=place[:, t:t + 1], axis=0),
                                        in_=XN[:, t, :], in_offset=None).then_inc(s.scattered, 16)
            if n == 0:
                pool.wait_ge(attn_w_in, 16 * 7)
                pool.tensor_copy(w_hi[:, :, :], w_raw[:, :, :]).then_inc(w_hi_set, 1)
                pool.wait_ge(w_hi_set, 1)
                pool.tensor_tensor(w_lo[:, :, :], w_raw[:, :, :], w_hi[:, :, :].bitcast(F32),
                                   ALU.subtract).then_inc(w_lo_set, 1)
            for r in range(RING):
                pool.wait_ge(s.y_stored[r], 16 * (NG // RING))
            pool.wait_ge(s.scattered, 16 * TILES)
            for t in range(TILES):
                pool.indirect_dma_start(out=XN[:, t, :], out_offset=None, in_=grouped_y,
                                        in_offset=bass.IndirectOffsetOnAxis(ap=place[:, t:t + 1], axis=0)
                                        ).then_inc(s.gathered[t // ROW], 16)

        GBANK = {1: (0, 1, 0, 1, 1, 0), 0: (0, 1, 0, 1, 0, 1)}
        WO_BANK, TX_BANK = 0, 1

        def pe_turn_x(pe, b, first=False):
            pe.wait_ge(xn_set, b + 1)
            if not first:
                pe.wait_ge(v_set, 4 * b - 1)
            for t in range(QT):
                mm = pe.transpose(bank[TX_BANK][:, t * P:(t + 1) * P], xn[:, t, :], ident)
            mm.then_inc(xT_mm, 1)

        def pe_project(pe, tau, half, m, first=False):
            kind, t = m // QT, m % QT
            bk = GBANK[half][m]
            if m == 0:
                pe.wait_ge(xT_lo_set, (tau - half) // 2 + 1 if isinstance(tau, int) else tau[1] + 1)
            n = tau if isinstance(tau, int) else tau[0]
            if m >= 2 and not (half == 1 and m >= 4):
                pe.wait_ge(rope_w, 4 * n + m - 1)
            elif half == 1 and m == 4:
                pe.wait_ge(rope_w, 4 * n + 4)
            elif half == 1 and m == 5:
                pe.wait_ge(rope_w, 4 * n + 3)
                if not first:
                    pe.wait_ge(wo_added, (n - 1) // 2 if isinstance(n, int) else tau[1])
            elif half == 1:
                pe.wait_ge(v_set, 2 * n - 1 + m)
            elif half == 0 and m == 0 and not first:
                pe.wait_ge(v_set, 2 * n)
            for a, (xs, ws) in enumerate(((xT_hi, w_hi), (xT_hi, w_lo), (xT_lo, w_hi))):
                mm = pe.matmul(bank[bk][:, :], xs[:, t * P:(t + 1) * P], ws[:, 2 * kind + half, :],
                               start=(a == 0), stop=(a == 2))
            mm.then_inc(proj_mm, 1)

        def pe_turn_qk(pe, n, half, j):
            if j == 0:
                pe.wait_ge(rot_set, 4 * n + 4)
            if not (isinstance(n, int) and n == 0 and j == 0):
                pe.wait_ge(qk_lo_set, 4 * n + j)
            for kind in range(2):
                for t in range(QT):
                    mm = pe.transpose(bank[6][:, (kind * QT + t) * P:(kind * QT + t + 1) * P],
                                      rot[:, kind, t, j * P:(j + 1) * P], ident)
            mm.then_inc(turn_mm, 1)

        def pe_scores(pe, b, h, first=False):
            half, i = h // HALF, h % HALF
            j, at = i // 2, HEAD * (i % 2)
            if i % 2 == 0:
                pe.wait_ge(qk_lo_set, 8 * b + 4 * half + j + 1)
            if not first:
                pe.wait_ge(exp_set, HEADS * b + h - 1)
            q = [a[at:at + HEAD, half, j, 0, :] for a in (qk_hi, qk_lo)]
            k = [a[at:at + HEAD, half, j, 1, :] for a in (qk_hi, qk_lo)]
            for t in range(QT):
                for a, (x1, x2) in enumerate(((0, 0), (0, 1), (1, 0))):
                    mm = pe.matmul(bank[2 + h % 2][:, t * SEQ:(t + 1) * SEQ], q[x1][:, t * P:(t + 1) * P], k[x2],
                                   start=(a == 0), stop=(a == 2))
            mm.then_inc(score_mm, 1)

        def pe_turn_e(pe, b, h, first=False):
            pe.wait_ge(prob_set, HEADS * b + h + 1)
            if not first:
                pe.wait_ge(et_set, HEADS * b + h - 1)
            for kt in range(QT):
                for t in range(QT):
                    mm = pe.transpose(bank[4 + h % 2][:, kt * SEQ + t * P:kt * SEQ + (t + 1) * P],
                                      E[:, h % 4, t, kt * P:(kt + 1) * P], ident)
            mm.then_inc(et_mm, 1)

        def pe_pv(pe, b, h, first=False):
            half, i = h % HEADS // HALF, h % HALF
            at = HEAD * (i % 2)
            pe.wait_ge(et_set, HEADS * b + h + 1)
            if i == 0:
                pe.wait_ge(v_set, 4 * b + 2 * half + 2)
            if i % 2 == 0 and not first:
                pe.wait_ge(ot_set, 8 * b + h // 2)
            for kt in range(QT):
                mm = pe.matmul(bank[7][at:at + HEAD, 0:SEQ], V[:, half, kt, i * HEAD:(i + 1) * HEAD],
                               ET[:, h % 2, kt * SEQ:(kt + 1) * SEQ], start=(kt == 0), stop=(kt == QT - 1))
            mm.then_inc(pv_mm, 1)

        def pe_wo(pe, b, b_prev, last=False):
            pe.wait_ge(ot_set, 8 * (b_prev + 1))
            if not last:
                pe.wait_ge(rope_w, 4 * (2 * b + 1) + 3)
            for t in range(QT):
                for j in range(HEADS // 2):
                    mm = pe.matmul(bank[WO_BANK][:, t * D:(t + 1) * D], OT[:, j, t * P:(t + 1) * P], Wo[:, j, :],
                                   start=(j == 0), stop=(j == HEADS // 2 - 1))
            mm.then_inc(wo_mm, 1)

        def pe_batch(pe, b, first=False, last=False):
            for half in range(2):
                prep = not (last and half == 1)
                tau = 2 * b + half + 1
                tgt = 1 - half
                tb = (tau, b + half)
                for i in range(HALF):
                    h = HALF * half + i
                    pe_scores(pe, b, h, first=first and h < 2)
                    if not (first and h < 2):
                        pe_turn_e(pe, b - 1 if h < 2 else b, (h - 2) % HEADS, first=first and h < 4)
                    if prep and i < 6:
                        pe_project(pe, tb, tgt, i, first=first)
                    if not (first and h < 3):
                        pe_pv(pe, b - 1 if h < 3 else b, (h - 3) % HEADS, first=first and h < 5)
                    if half == 0 and i == 3 and not first:
                        pe_wo(pe, b, b - 1)
                    if half == 0 and i == 6 and not last:
                        pe_turn_x(pe, b + 1)
                    if prep and i >= 4:
                        pe_turn_qk(pe, tau, tgt, i - 4)

        def attention_tensor(pe):
            pe.wait_ge(w_lo_set, 1)
            pe_turn_x(pe, 0, first=True)
            for m in range(6):
                pe_project(pe, 0, 0, m, first=True)
            for j in range(PAIRS):
                pe_turn_qk(pe, 0, 0, j)
            pe_batch(pe, 0, first=True)
            with pe.Fori(1, BATCH - 1) as b:
                pe_batch(pe, b)
            pe_batch(pe, BATCH - 1, last=True)
            pe_turn_e(pe, BATCH - 1, HEADS - 2)
            pe_pv(pe, BATCH - 1, HEADS - 3)
            pe_turn_e(pe, BATCH - 1, HEADS - 1)
            pe_pv(pe, BATCH - 1, HEADS - 2)
            pe_pv(pe, BATCH - 1, HEADS - 1)
            pe_wo(pe, BATCH, BATCH - 1, last=True)

        def act_hi(act, n, half, j):
            act.wait_ge(turn_mm, 4 * n + j + 1)
            act.activation(qk_hi[:, half, j, :, :], bank[6][:, :].rearrange("p (k s) -> p k s", k=2),
                           ACT.Copy).then_inc(qk_hi_set, 1)

        def act_v(act, n, half, t):
            act.wait_ge(proj_mm, 6 * n + 5 + t)
            act.activation(V[:, half, t, :], bank[GBANK[half][4 + t]][:, :], ACT.Copy).then_inc(v_set, 1)

        def act_x_hi(act, b):
            act.wait_ge(xT_mm, b + 1)
            act.activation(xT_hi[:, :], bank[TX_BANK][:, 0:SEQ], ACT.Copy).then_inc(xT_hi_set, 1)

        def act_ot(act, b, j, first=False):
            act.wait_ge(pv_mm, HEADS * b + 2 * j + 2)
            if not first:
                act.wait_ge(wo_mm, b)
            act.activation(OT[:, j, :], bank[7][:, 0:SEQ], ACT.Copy).then_inc(ot_set, 1)

        def act_et(act, b, h, first=False):
            act.wait_ge(et_mm, HEADS * b + h + 1)
            if not first:
                act.wait_ge(pv_mm, HEADS * b + h - 1)
            act.activation(ET[:, h % 2, :], bank[4 + h % 2][:, :], ACT.Copy).then_inc(et_set, 1)

        def act_exp(act, b, h, first=False):
            act.wait_ge(max_set, HEADS * b + h + 1)
            if not first:
                act.wait_ge(et_mm, HEADS * b + h - 3)
            for t in range(QT):
                ins = act.activation(E[:, h % 4, t, :], bank[2 + h % 2][:, t * SEQ:(t + 1) * SEQ], ACT.Exp,
                                     bias=negmax[:, h % 2, t:t + 1], accum_out=total[:, h % 2, t:t + 1])
            ins.then_inc(exp_set, 1)

        def act_batch(act, b, first=False, last=False):
            for half in range(2):
                prep = not (last and half == 1)
                tau = 2 * b + half + 1
                tgt = 1 - half
                for i in range(HALF):
                    h = HALF * half + i
                    if i == 0:
                        act_hi(act, 2 * b + half, half, 3)
                    if prep and i >= 5:
                        act_hi(act, tau, tgt, i - 5)
                    if not (first and h < 1):
                        act_exp(act, b - 1 if h < 1 else b, (h - 1) % HEADS, first=first and h < 5)
                    if h % 2 == 1 and not (first and h < 5):
                        act_ot(act, b - 1 if h < 5 else b, (h - 5) % HEADS // 2, first=first)
                    if not (first and h < 2):
                        act_et(act, b - 1 if h < 2 else b, (h - 2) % HEADS, first=first and h < 4)
                    if prep and 4 <= i < 6:
                        act_v(act, tau, tgt, i - 4)
                    if half == 0 and i == 6 and not last:
                        act_x_hi(act, b + 1)

        def attention_scalar(act):
            act.wait_ge(ln2_var, 1)
            act.activation(ln[:, 1, :], ln[:, 0, :], ACT.Sqrt).then_inc(ln2_sqrt, 1)
            act_x_hi(act, 0)
            for t in range(QT):
                act_v(act, 0, 0, t)
            for j in range(PAIRS - 1):
                act_hi(act, 0, 0, j)
            act_batch(act, 0, first=True)
            with act.Fori(1, BATCH - 1) as b:
                act_batch(act, b)
            act_batch(act, BATCH - 1, last=True)
            act_exp(act, BATCH - 1, HEADS - 1)
            act_et(act, BATCH - 1, HEADS - 2)
            act_ot(act, BATCH - 1, HEADS // 2 - 2)
            act_et(act, BATCH - 1, HEADS - 1)
            act_ot(act, BATCH - 1, HEADS // 2 - 1)

        def dve_xn(dve, b, first=False):
            if not first:
                dve.wait_ge(xT_mm, b)
            for t in range(QT):
                tile = b * QT + t
                ins = dve.tensor_scalar(xn[:, t, :], X[:, bass.ds(tile, 1), :].squeeze(1) if not isinstance(b, int) else X[:, tile, :],
                                        mv[:, bass.ds(tile, 1), 0:1].squeeze(1), rstd[:, bass.ds(tile, 1)],
                                        ALU.subtract, ALU.mult)
            ins.then_inc(xn_set, 1)

        def dve_x_lo(dve, b):
            dve.wait_ge(xT_hi_set, b + 1)
            dve.tensor_tensor(xT_lo[:, :], bank[TX_BANK][:, 0:SEQ], xT_hi[:, :].bitcast(F32),
                              ALU.subtract).then_inc(xT_lo_set, 1)

        def dve_rope(dve, n, half, m, first=False):
            kind, t = m // QT, m % QT
            dve.wait_ge(proj_mm, 6 * n + m + 1)
            if not (first and m < 2):
                dve.wait_ge(rot_set, 4 * n + m - 1)
            src = bank[GBANK[half][m]][:, :]
            pb = m % 2
            dve.tensor_tensor(rot_u[:, pb, :].rearrange("p (h d) -> p h d", d=HEAD),
                              src.rearrange("p (h d) -> p h d", d=HEAD),
                              table(kind, 0, t).unsqueeze(1).to_broadcast([P, HALF, HEAD]), ALU.mult)
            dve.tensor_tensor(rot_w[:, pb, :].rearrange("p (h j d) -> p h j d", j=2, h=HALF)[:, :, ::-1, :],
                              src.rearrange("p (h j d) -> p h j d", j=2, h=HALF),
                              table(kind, 1, t).rearrange("p (j d) -> p j d", j=2).unsqueeze(1)
                              .to_broadcast([P, HALF, 2, HEAD // 2]), ALU.mult).then_inc(rope_w, 1)

        def dve_lo(dve, n, half, j):
            dve.wait_ge(qk_hi_set, 4 * n + j + 1)
            dve.tensor_tensor(qk_lo[:, half, j, :, :], bank[6][:, :].rearrange("p (k s) -> p k s", k=2),
                              qk_hi[:, half, j, :, :].bitcast(F32), ALU.subtract).then_inc(qk_lo_set, 1)

        def dve_max(dve, b, h):
            dve.wait_ge(score_mm, HEADS * b + h + 1)
            dve.tensor_reduce(negmax[:, h % 2, :], bank[2 + h % 2][:, :].rearrange("p (t s) -> p t s", t=QT),
                              AX.X, ALU.max, negate=True).then_inc(max_set, 1)

        def dve_recip(dve, b, h):
            dve.wait_ge(exp_set, HEADS * b + h + 1)
            dve.reciprocal(recip[:, h % 2, :], total[:, h % 2, :]).then_inc(recip_set, 1)

        def dve_prob(dve, b, h):
            dve.wait_ge(recip_set, HEADS * b + h + 1)
            for t in range(QT):
                ins = dve.tensor_scalar(E[:, h % 4, t, :], E[:, h % 4, t, :], recip[:, h % 2, t:t + 1], None, ALU.mult)
            ins.then_inc(prob_set, 1)

        def dve_wo(dve, b):
            dve.wait_ge(wo_mm, b + 1)
            xs = X[:, bass.ds(b * QT, QT), :]
            dve.tensor_tensor(xs, bank[WO_BANK][:, 0:QT * D].rearrange("p (t d) -> p t d", t=QT), xs,
                              ALU.add).then_inc(wo_added, 1)

        def dve_batch(dve, b, first=False, last=False):
            for half in range(2):
                prep = not (last and half == 1)
                tau = 2 * b + half + 1
                tgt = 1 - half
                for i in range(HALF):
                    h = HALF * half + i
                    pb, ph = (b - 1 if h < 1 else b), (h - 1) % HEADS
                    if i == 0:
                        dve_lo(dve, 2 * b + half, half, 3)
                    if prep and i >= 5:
                        dve_lo(dve, tau, tgt, i - 5)
                    dve_max(dve, b, h)
                    if not (first and h < 1):
                        dve_recip(dve, pb, ph)
                    if not (first and h < 1):
                        dve_prob(dve, pb, ph)
                    if half == 0 and i == 4 and not first:
                        dve_wo(dve, b - 1)
                    if half == 0 and i == 4 and not last:
                        dve_xn(dve, b + 1)
                    if prep and i < 4:
                        dve_rope(dve, tau, tgt, i)
                    if half == 0 and i == 7 and not last:
                        dve_x_lo(dve, b + 1)

        def attention_vector(dve):
            for t in range(TILES):
                ins = dve.bn_stats(stats[:, t, :], X[:, t, :])
            link(dve, ins)
            aggregate(dve)
            norm_stats(dve, ln2_var, ln2_sqrt)
            dve_xn(dve, 0, first=True)
            dve_x_lo(dve, 0)
            for m in range(4):
                dve_rope(dve, 0, 0, m, first=True)
            for j in range(PAIRS - 1):
                dve_lo(dve, 0, 0, j)
            dve_batch(dve, 0, first=True)
            with dve.Fori(1, BATCH - 1) as b:
                dve_batch(dve, b)
            dve_batch(dve, BATCH - 1, last=True)
            dve_recip(dve, BATCH - 1, HEADS - 1)
            dve_prob(dve, BATCH - 1, HEADS - 1)
            dve_wo(dve, BATCH - 1)
            dve.wait_ge(wo_added, BATCH)

        def pool_rot(pool, n, m):
            pool.wait_ge(rope_w, 4 * n + m + 1)
            if m == 0 and not (isinstance(n, int) and n == 0):
                pool.wait_ge(turn_mm, 4 * n)
            pool.tensor_tensor(rot[:, m // QT, m % QT, :], rot_u[:, m % 2, :], rot_w[:, m % 2, :],
                               ALU.add).then_inc(rot_set, 1)

        def attention_gpsimd(pool):
            pool.wait_ge(ffn[0].added, TILES // ROW)
            for m in range(4):
                pool_rot(pool, 0, m)
            with pool.Fori(1, 2 * BATCH) as n:
                for m in range(4):
                    pool_rot(pool, n, m)

        @block.sync
        def _(sp):
            sp.dma_start(con[:, :], consts).then_inc(con_in, 16)
            for g in range(4):
                sp.dma_start(X[:, 8 * g:8 * g + 8, :], x_t[:, 8 * g:8 * g + 8, :]).then_inc(x_in[g], 16)
            sp.dma_start(Wr[:, :], wr).then_inc(small_in, 16)
            sp.dma_start(br_all[:, :], br.rearrange("(a e) -> a e", a=1).to_broadcast([P, EXPERTS])).then_inc(small_in, 16)
            sp.dma_start(b1_rows[:, :], b1.rearrange("e (c p) -> (e c) p", p=P)).then_inc(small_in, 16)
            sp.dma_start(b2_all[:, :], b2.rearrange("(a e) d -> a (e d)", a=1).to_broadcast([P, EXPERTS * D])
                         ).then_inc(small_in, 16)
            sp.wait_ge(const_set, 1)
            sp.dma_start(grouped_x.rearrange("(n p) d -> p n d", p=P),
                         zero[:, :].unsqueeze(1).to_broadcast([P, NG, D])).then_inc(zero_fill, 16)
            sp.dma_start(W1[:, :].rearrange("p (e f) -> p e f", e=EXPERTS), w1.rearrange("e p f -> p e f")
                         ).then_inc(ffn_w_in, 16)
            sp.dma_start(W2[:, :].rearrange("p (e c d) -> p e c d", e=EXPERTS, c=FC),
                         w2.rearrange("e (c p) d -> p e c d", p=P)).then_inc(ffn_w_in, 16)
            for k, w in enumerate((wq, wk, wv)):
                for half in range(2):
                    sp.dma_start(w_raw[:, 2 * k + half, :], w[:, 512 * half:512 * half + 512]).then_inc(attn_w_in, 16)
            sp.dma_start(Wo[:, :, :], wo.rearrange("(j p) d -> p j d", p=P)).then_inc(attn_w_in, 16)
            ffn_load_store(sp, ffn[0])
            ffn_load_store(sp, ffn[1])
            for g in range(TILES // ROW):
                sp.wait_ge(ffn[1].added, g + 1)
                sp.dma_start(out_t[:, ROW * g:ROW * g + ROW, :], X[:, ROW * g:ROW * g + ROW, :]).then_inc(out_done, 16)
            sp.wait_ge(out_done, 16 * (TILES // ROW))

        @block.tensor
        def _(pe):
            pe.wait_ge(con_in, 16)
            ffn_tensor(pe, ffn[0], 0)
            attention_tensor(pe)
            ffn_tensor(pe, ffn[1], 1)

        @block.scalar
        def _(act):
            ffn_scalar(act, ffn[0])
            attention_scalar(act)
            ffn_scalar(act, ffn[1])

        @block.vector
        def _(dve):
            dve.memset(zero[:, :], 0.0).then_inc(const_set, 1)
            dve.memset(ones[:, :], 1.0).then_inc(const_set, 1)
            ffn_vector(dve, ffn[0], 0)
            dve.wait_ge(ffn[0].added, TILES // ROW)
            attention_vector(dve)
            ffn_vector(dve, ffn[1], 1)

        @block.gpsimd
        def _(pool):
            ffn_gpsimd(pool, ffn[0], 0)
            attention_gpsimd(pool)
            ffn_gpsimd(pool, ffn[1], 1)


def even_odd(w):
    return w.reshape(D, HEADS, HEAD // 2, 2).transpose(0, 1, 3, 2).reshape(D, HEADS * HEAD)


def kernel(L0_attn_x, L0_attn_Wq, L0_attn_Wk, L0_attn_Wv, L0_attn_Wo, L0_ffn_Wr, L0_ffn_br, L0_ffn_W1, L0_ffn_b1,
           L0_ffn_W2, L0_ffn_b2):
    import numpy as np
    import concourse.bacc as bacc
    from concourse.bass_utils import run_bass_kernel_spmd

    arrays = {
        "x": np.asarray(L0_attn_x), "wq": even_odd(np.asarray(L0_attn_Wq)), "wk": even_odd(np.asarray(L0_attn_Wk)),
        "wv": np.asarray(L0_attn_Wv), "wo": np.asarray(L0_attn_Wo), "wr": np.asarray(L0_ffn_Wr),
        "br": np.asarray(L0_ffn_br), "w1": np.asarray(L0_ffn_W1), "b1": np.asarray(L0_ffn_b1),
        "w2": np.asarray(L0_ffn_W2), "b2": np.asarray(L0_ffn_b2), "consts": constants(),
    }
    arrays = {f"in_{name}": np.ascontiguousarray(a) for name, a in arrays.items()}
    nc = bacc.Bacc("TRN2", target_bir_lowering=False, num_devices=1)
    args = [nc.dram_tensor(name, a.shape, mybir.dt.from_np(a.dtype), kind="ExternalInput").ap()
            for name, a in arrays.items()]
    out = nc.dram_tensor("out_0", (BATCH, SEQ, D), F32, kind="ExternalOutput").ap()
    macaron_kernel(nc, *args, out)
    r = run_bass_kernel_spmd(nc, [arrays], core_ids=[0])
    return r.results[0]["out_0"]
```

```python
from contextlib import ExitStack

import concourse.bass as bass
from concourse import mybir

F32 = mybir.dt.float32
F32R = mybir.dt.float32r
I32 = mybir.dt.int32
U32 = mybir.dt.uint32
ALU = mybir.AluOpType
ACT = mybir.ActivationFunctionType
AX = mybir.AxisListType

P = 128
BATCH, SEQ, D = 16, 256, 128
HEADS, HEAD = 16, 64
EXPERTS, DFF = 8, 512
TILES = BATCH * SEQ // P
QT = SEQ // P
NG = TILES + EXPERTS
FC = DFF // P
HALF = HEADS // 2
PAIRS = HALF // 2
EPS = 1e-5
ROW = 4
RING = 4

C_ID, C_LOW, C_ONE = 0, P, 2 * P
C_ROPE = 3 * P
C_DESC = C_ROPE + 4 * QT * HEAD
C_THR = C_DESC + EXPERTS
C_TIX = C_THR + TILES
C_ALL = C_TIX + NG


def constants():
    import numpy as np

    f = np.float32
    c = np.zeros((P, C_ALL), f)
    c[:, C_ID:C_ID + P] = np.eye(P, dtype=f)
    c[:, C_LOW:C_LOW + P] = np.triu(np.ones((P, P), f), 1)
    c[:, C_ONE:C_ONE + P] = 1
    pos = np.arange(SEQ, dtype=f)
    i = np.arange(HEAD // 2, dtype=f)
    cos, sin = [], []
    for s in (1.0, 4.0, 16.0):
        freq = f(1.0) / np.power(f(10000.0 * s), f(2.0) * i / f(HEAD), dtype=f)
        ang = pos[:, None] * freq[None, :]
        cos.append(np.cos(ang))
        sin.append(np.sin(ang))
    cos = np.mean(np.stack(cos), 0, dtype=f)
    sin = np.mean(np.stack(sin), 0, dtype=f)
    scale = f(HEAD) ** f(-0.5)
    for n, (a, b) in enumerate(((cos, cos), (sin, -sin))):
        t = np.concatenate([a, b], 1).reshape(QT, P, HEAD).transpose(1, 0, 2).reshape(P, QT * HEAD)
        at = C_ROPE + n * QT * HEAD
        c[:, at:at + QT * HEAD] = t * scale
        c[:, at + 2 * QT * HEAD:at + 3 * QT * HEAD] = t
    c[:, C_DESC:C_DESC + EXPERTS] = np.arange(EXPERTS, 0, -1)
    c[:, C_THR:C_THR + TILES] = P * np.arange(TILES)
    c[:, C_TIX:C_TIX + NG] = np.arange(NG)
    return c


def macaron_kernel(nc, x, wq, wk, wv, wo, wr, br, w1, b1, w2, b2, consts, out):
    x_t = x.rearrange("b (n p) d -> p (b n) d", p=P)
    out_t = out.rearrange("b (n p) d -> p (b n) d", p=P)
    grouped_x = nc.dram_tensor("grouped_x", [NG * P, D], F32).ap()
    grouped_y = nc.dram_tensor("grouped_y", [NG * P, D], F32).ap()

    with ExitStack() as ctx:
        def sb(name, shape, dt=F32):
            return ctx.enter_context(nc.sbuf_tensor(name, shape, dt))

        def sem(name):
            return ctx.enter_context(nc.semaphore(name))

        bank = [ctx.enter_context(nc.psum_tensor(f"bank{n}", [P, 512], F32)) for n in range(8)]

        con = sb("con", [P, C_ALL])
        X = sb("X", [P, TILES, D])
        XN = sb("XN", [P, TILES, D])
        W1 = sb("W1", [P, EXPERTS * DFF])
        W2 = sb("W2", [P, EXPERTS * FC * D])
        b1_rows = sb("b1_rows", [EXPERTS * FC, P])
        b1_col = sb("b1_col", [P, EXPERTS * FC])
        b2_all = sb("b2_all", [P, EXPERTS * D])
        Wr = sb("Wr", [P, EXPERTS])
        br_all = sb("br_all", [P, EXPERTS])
        zero = sb("zero", [P, D])
        ones = sb("ones", [P, TILES * EXPERTS])
        w_raw = sb("w_raw", [P, 6, 512])
        w_hi = sb("w_hi", [P, 6, 512], F32R)
        w_lo = sb("w_lo", [P, 6, 512], F32R)
        Wo = sb("Wo", [P, HEADS // 2, D])
        stats = sb("stats", [P, TILES, 6])
        mv = sb("mv", [P, TILES, 2])
        ln = sb("ln", [P, 6, TILES])
        rstd = ln[:, 5, :]
        XNT = sb("XNT", [P, 2, ROW * P])
        R = sb("R", [P, 8, TILES * EXPERTS])
        small = sb("small", [P, 12, TILES])
        first_le = sb("first_le", [P, NG, EXPERTS - 1])
        expert_f = sb("expert_f", [P, NG])
        expert_of = sb("expert_of", [P, NG], I32)
        place = sb("place", [P, TILES], U32)
        half_gate = sb("half_gate", [P, TILES])
        XG = sb("XG", [P, RING, D])
        XT = sb("XT", [P, 2, P])
        shared = sb("shared", [P, 4 * DFF])
        Hs = shared[:, 0:2 * DFF].rearrange("p (r f) -> p r f", r=2)
        HT = shared[:, 2 * DFF:4 * DFF].rearrange("p (r c t) -> p r c t", r=2, c=FC)
        Y = sb("Y", [P, RING, D])
        xn = sb("xn", [P, QT, D])
        xT_hi = sb("xT_hi", [P, SEQ], F32R)
        xT_lo = sb("xT_lo", [P, SEQ], F32R)
        rot_u = sb("rot_u", [P, 2, 512])
        rot_w = sb("rot_w", [P, 2, 512])
        rot = XN[:, 0:2 * QT * 4, :].rearrange("p (k t c) d -> p k t (c d)", k=2, t=QT)
        qk_hi = sb("qk_hi", [P, 2, PAIRS, 2, SEQ], F32R)
        qk_lo = sb("qk_lo", [P, 2, PAIRS, 2, SEQ], F32R)
        V = sb("V", [P, 2, QT, 512])
        negmax = sb("negmax", [P, 2, QT])
        total = sb("total", [P, 2, QT])
        recip = sb("recip", [P, 2, QT])
        E = sb("E", [P, 4, QT, SEQ])
        ET = sb("ET", [P, 2, QT * SEQ])
        OT = shared[:, :].rearrange("p (j s) -> p j s", j=HEADS // 2)

        ident = con[:, C_ID:C_ID + P]
        lower = con[:, C_LOW:C_LOW + P]
        ones_sq = con[:, C_ONE:C_ONE + P]

        def table(kind, which, tt):
            at = C_ROPE + ((2 * kind + which) * QT + tt) * HEAD
            return con[:, at:at + HEAD]

        x_in = [sem(f"x_in{n}") for n in range(4)]
        con_in = sem("con_in")
        small_in = sem("small_in")
        ffn_w_in = sem("ffn_w_in")
        attn_w_in = sem("attn_w_in")
        const_set = sem("const_set")
        zero_fill = sem("zero_fill")
        w_hi_set = sem("w_hi_set")
        w_lo_set = sem("w_lo_set")
        b1_turned = sem("b1_turned")
        b1_set = sem("b1_set")
        dve_step = sem("dve_step")
        out_done = sem("out_done")
        steps = [0]

        def link(eng, ins):
            ins.then_inc(dve_step, 1)
            steps[0] += 1
            eng.wait_ge(dve_step, steps[0])

        class Sems:
            pass

        def ffn_sems(n):
            s = Sems()
            s.var_ready = sem(f"f{n}_var_ready")
            s.sqrt_ready = sem(f"f{n}_sqrt_ready")
            s.normed = sem(f"f{n}_normed")
            s.turned = sem(f"f{n}_turned")
            s.turned_out = sem(f"f{n}_turned_out")
            s.logits = sem(f"f{n}_logits")
            s.shifted = sem(f"f{n}_shifted")
            s.exped = sem(f"f{n}_exped")
            s.onehot = sem(f"f{n}_onehot")
            s.ranked = sem(f"f{n}_ranked")
            s.routed = sem(f"f{n}_routed")
            s.scattered = sem(f"f{n}_scattered")
            s.xg_in = [sem(f"f{n}_xg_in{r}") for r in range(RING)]
            s.xt_mm = sem(f"f{n}_xt_mm")
            s.xt_out = sem(f"f{n}_xt_out")
            s.h_mm = sem(f"f{n}_h_mm")
            s.h_out = sem(f"f{n}_h_out")
            s.ht_mm = sem(f"f{n}_ht_mm")
            s.ht_out = sem(f"f{n}_ht_out")
            s.y_mm = sem(f"f{n}_y_mm")
            s.y_out = sem(f"f{n}_y_out")
            s.y_stored = [sem(f"f{n}_y_stored{r}") for r in range(RING)]
            s.gathered = [sem(f"f{n}_gathered{r}") for r in range(TILES // ROW)]
            s.added = sem(f"f{n}_added")
            return s

        ffn = [ffn_sems(0), ffn_sems(1)]

        ln2_var = sem("ln2_var")
        ln2_sqrt = sem("ln2_sqrt")
        xn_set = sem("xn_set")
        xT_mm = sem("xT_mm")
        xT_hi_set = sem("xT_hi_set")
        xT_lo_set = sem("xT_lo_set")
        proj_mm = sem("proj_mm")
        rope_w = sem("rope_w")
        rot_set = sem("rot_set")
        v_set = sem("v_set")
        turn_mm = sem("turn_mm")
        qk_hi_set = sem("qk_hi_set")
        qk_lo_set = sem("qk_lo_set")
        score_mm = sem("score_mm")
        max_set = sem("max_set")
        exp_set = sem("exp_set")
        recip_set = sem("recip_set")
        prob_set = sem("prob_set")
        et_mm = sem("et_mm")
        et_set = sem("et_set")
        pv_mm = sem("pv_mm")
        ot_set = sem("ot_set")
        wo_mm = sem("wo_mm")
        wo_added = sem("wo_added")
        attn_done = wo_added

        block = ctx.enter_context(nc.Block())

        def ffn_load_store(sp, s):
            def load(j, r, free):
                if free is not None:
                    sp.wait_ge(s.xt_mm, free)
                sp.dma_start(XG[:, r, :], grouped_x[bass.ds(j * P, P), :]).then_inc(s.xg_in[r], 16)

            def store(j, r):
                sp.wait_ge(s.y_out, j + 1)
                sp.dma_start(grouped_y[bass.ds(j * P, P), :], Y[:, r, :]).then_inc(s.y_stored[r], 16)

            sp.wait_ge(s.scattered, 16 * TILES)
            for j in range(2 * RING):
                load(j, j % RING, j - RING + 1 if j >= RING else None)
            with sp.Fori(2, NG // RING) as q:
                for r in range(RING):
                    load(q * RING + r, r, q * RING + (r - RING + 1))
                    store(q * RING + (r - 2 * RING), r)
            for j in range(NG - 2 * RING, NG):
                store(j, j % RING)

        def ffn_tensor(pe, s, n):
            for g in range(TILES // ROW):
                pe.wait_ge(s.normed, ROW * (g + 1))
                if g >= 2:
                    pe.wait_ge(s.turned_out, g - 1)
                for k in range(ROW):
                    t = g * ROW + k
                    mm = pe.transpose(bank[g % 2][:, k * P:(k + 1) * P], XN[:, t, :], ident)
                mm.then_inc(s.turned, 1)
                if g == 0 and n == 0:
                    pe.wait_ge(small_in, 16 * 4)
                    pe.transpose(bank[4][:, 0:EXPERTS * FC], b1_rows[:, :],
                                 con[0:EXPERTS * FC, C_ID:C_ID + EXPERTS * FC]).then_inc(b1_turned, 1)
                if g >= 1:
                    logits(pe, s, g - 1)
            logits(pe, s, TILES // ROW - 1)
            pe.wait_ge(s.onehot, 1)
            onehot = R[:, 3, :]
            pe.matmul(bank[3][:, 0:TILES * EXPERTS], lower, onehot, start=True, stop=True)
            pe.matmul(bank[4][:, 0:TILES * EXPERTS], ones_sq, onehot, start=True, stop=True).then_inc(s.ranked, 1)

            def turn_x(j, r, q):
                pe.wait_ge(s.xg_in[r], (q + 1) * 16)
                if not (isinstance(j, int) and j == 0):
                    pe.wait_ge(s.xt_out, j)
                pe.transpose(bank[0][:, 0:P], XG[:, r, :], ident).then_inc(s.xt_mm, 1)

            def slot(q, r, w1=True, th=True, tx=True, w2=True, expert=(None, None)):
                j, p = q * RING + r, r % 2
                e = None
                if w1:
                    e = pe.value_load(expert_of[0:1, bass.ds(j, 1)], min_val=0, max_val=EXPERTS - 1)
                    pe.wait_ge(s.xt_out, j + 1)
                    if not (isinstance(j, int) and j < 2):
                        pe.wait_ge(s.h_out, j - 1)
                    pe.matmul(bank[1 + p][:, :], XT[:, p, :], W1[:, bass.ds(e * DFF, DFF)],
                              start=True, stop=True).then_inc(s.h_mm, 1)
                if th:
                    pe.wait_ge(s.h_out, j)
                    if not (isinstance(j, int) and j < 3):
                        pe.wait_ge(s.ht_out, j - 2)
                    for c in range(FC):
                        mm = pe.transpose(bank[3 + (1 - p)][:, c * P:(c + 1) * P],
                                          Hs[:, 1 - p, c * P:(c + 1) * P], ident)
                    mm.then_inc(s.ht_mm, 1)
                if tx:
                    turn_x(j + 2, (r + 2) % RING, q + (r + 2) // RING)
                if w2:
                    e2 = expert[1]
                    if e2 is None:
                        e2 = pe.value_load(expert_of[0:1, bass.ds(j - 2, 1)], min_val=0, max_val=EXPERTS - 1)
                    pe.wait_ge(s.ht_out, j - 1)
                    if not (isinstance(j, int) and j < 4):
                        pe.wait_ge(s.y_out, j - 3)
                    for c in range(FC):
                        mm = pe.matmul(bank[5 + p][:, 0:D], HT[:, p, c, :],
                                       W2[:, bass.ds(e2 * (FC * D) + c * D, D)],
                                       start=(c == 0), stop=(c == FC - 1))
                    mm.then_inc(s.y_mm, 1)
                return e, expert[0]

            pe.wait_ge(s.routed, 1)
            if n == 0:
                pe.wait_ge(ffn_w_in, 32)
            turn_x(0, 0, 0)
            turn_x(1, 1, 0)
            last = (None, None)
            for j in range(RING):
                last = slot(0, j, th=j >= 1, w2=j >= 2, expert=last)
            with pe.Fori(1, NG // RING - 1) as q:
                last = (None, None)
                for r in range(RING):
                    last = slot(q, r, expert=last)
            last = (None, None)
            for r in range(RING):
                last = slot(NG // RING - 1, r, tx=r < 2, expert=last)
            last = slot(NG // RING, 0, w1=False, tx=False, expert=last)
            slot(NG // RING, 1, w1=False, th=False, tx=False, expert=last)

        def logits(pe, s, g):
            pe.wait_ge(s.turned_out, g + 1)
            for k in range(ROW):
                t = g * ROW + k
                mm = pe.matmul(bank[2][:, t * EXPERTS:(t + 1) * EXPERTS], XNT[:, g % 2, k * P:(k + 1) * P],
                               Wr[:, :], start=True, stop=True)
            mm.then_inc(s.logits, 1)

        def ffn_scalar(act, s):
            act.wait_ge(s.var_ready, 1)
            act.activation(ln[:, 1, :], ln[:, 0, :], ACT.Sqrt).then_inc(s.sqrt_ready, 1)
            for g in range(TILES // ROW):
                act.wait_ge(s.turned, g + 1)
                if g >= 2:
                    act.wait_ge(s.logits, g - 1)
                act.activation(XNT[:, g % 2, :], bank[g % 2][:, :], ACT.Copy).then_inc(s.turned_out, 1)
            act.wait_ge(s.shifted, 1)
            act.activation(R[:, 4, :], R[:, 1, :], ACT.Exp).then_inc(s.exped, 1)

            def copy_x(j, p):
                act.wait_ge(s.xt_mm, j + 1)
                if not (isinstance(j, int) and j < 2):
                    act.wait_ge(s.h_mm, j - 1)
                act.activation(XT[:, p, :], bank[0][:, 0:P], ACT.Copy).then_inc(s.xt_out, 1)

            def slot(j, p, xt=True):
                act.wait_ge(s.h_mm, j + 1)
                if not (isinstance(j, int) and j < 2):
                    act.wait_ge(s.ht_mm, j - 1)
                act.activation(Hs[:, p, :], bank[1 + p][:, :], ACT.Copy).then_inc(s.h_out, 1)
                if xt:
                    copy_x(j + 2, p)

            copy_x(0, 0)
            copy_x(1, 1)
            slot(0, 0)
            slot(1, 1)
            with act.Fori(1, NG // 2 - 1) as q:
                for p in range(2):
                    slot(q * 2 + p, p)
            slot(NG - 2, 0, xt=False)
            slot(NG - 1, 1, xt=False)

        def norm_stats(dve, s_var, s_sqrt):
            link(dve, dve.tensor_scalar(ln[:, 0, :], mv[:, :, 1], EPS, None, ALU.add))
            dve.drain().then_inc(s_var, 1)
            dve.wait_ge(s_sqrt, 1)
            link(dve, dve.reciprocal(ln[:, 2, :], ln[:, 1, :]))
            link(dve, dve.tensor_tensor(ln[:, 3, :], ln[:, 0, :], ln[:, 2, :], ALU.mult))
            link(dve, dve.tensor_tensor(ln[:, 4, :], ln[:, 1, :], ln[:, 3, :], ALU.add))
            link(dve, dve.tensor_scalar(ln[:, 3, :], ln[:, 4, :], 0.5, None, ALU.mult))
            link(dve, dve.reciprocal(rstd, ln[:, 3, :]))

        def aggregate(dve):
            for t in range(TILES):
                ins = dve.bn_aggr(mv[:, t, :], stats[:, t, :])
            link(dve, ins)

        def ffn_vector(dve, s, n):
            if n == 0:
                for g in range(4):
                    dve.wait_ge(x_in[g], 16)
                    for t in range(8 * g, 8 * g + 8):
                        ins = dve.bn_stats(stats[:, t, :], X[:, t, :])
            else:
                for t in range(TILES):
                    ins = dve.bn_stats(stats[:, t, :], X[:, t, :])
            link(dve, ins)
            aggregate(dve)
            norm_stats(dve, s.var_ready, s.sqrt_ready)
            for t in range(TILES):
                dve.tensor_scalar(XN[:, t, :], X[:, t, :], mv[:, t, 0:1], rstd[:, t:t + 1],
                                  ALU.subtract, ALU.mult).then_inc(s.normed, 1)
            if n == 0:
                dve.wait_ge(b1_turned, 1)
                dve.tensor_copy(b1_col[:, :], bank[4][:, 0:EXPERTS * FC]).then_inc(b1_set, 1)
                dve.wait_ge(b1_set, 1)
                dve.wait_ge(con_in, 16)
                dve.wait_ge(small_in, 16 * 4)

            def te(ap):
                return ap.rearrange("p (t e) -> p t e", e=EXPERTS)

            def et(ap):
                return ap.rearrange("p (e t) -> p e t", t=TILES)

            def by_tile(v):
                return v.unsqueeze(2).to_broadcast([P, TILES, EXPERTS])

            full = [P, TILES, EXPERTS]
            desc = con[:, C_DESC:C_DESC + EXPERTS].unsqueeze(1).to_broadcast(full)
            lg, sh, cand, oh, ex, cnt, inc, exc = (R[:, k, :] for k in range(8))
            mx, cm, se = small[:, 0, :], small[:, 1, :], small[:, 2, :]
            n_of, n_tiles, upto, before, adj = (small[:, k, 0:EXPERTS] for k in range(3, 8))
            place_f = small[:, 8, :]
            dve.wait_ge(s.logits, TILES // ROW)
            link(dve, dve.tensor_tensor(te(lg), te(bank[2][:, 0:TILES * EXPERTS]),
                                        br_all[:, :].unsqueeze(1).to_broadcast(full), ALU.add))
            link(dve, dve.tensor_reduce(mx, te(lg), AX.X, ALU.max))
            dve.tensor_tensor(te(sh), te(lg), by_tile(mx), ALU.subtract).then_inc(s.shifted, 1)
            link(dve, dve.tensor_tensor(te(cand), te(lg), by_tile(mx), ALU.is_equal))
            link(dve, dve.tensor_tensor(te(cand), te(cand), desc, ALU.mult))
            link(dve, dve.tensor_reduce(cm, te(cand), AX.X, ALU.max))
            dve.tensor_tensor(te(oh), te(cand), by_tile(cm), ALU.is_equal).then_inc(s.onehot, 1)
            dve.wait_ge(s.exped, 1)
            link(dve, dve.tensor_reduce(se, te(ex), AX.X, ALU.add))
            link(dve, dve.reciprocal(small[:, 9, :], se))
            link(dve, dve.tensor_scalar(half_gate[:, :], small[:, 9, :], 0.5, None, ALU.mult))
            dve.wait_ge(s.ranked, 1)
            link(dve, dve.tensor_copy(et(cnt), te(bank[4][:, 0:TILES * EXPERTS]).rearrange("p t e -> p e t")))
            dve.wait_ge(const_set, 2)
            link(dve, dve.tensor_tensor_scan(inc, ones[:, :], cnt, 0.0, ALU.mult, ALU.add))
            link(dve, dve.tensor_tensor(exc, inc, cnt, ALU.subtract))
            link(dve, dve.tensor_reduce(n_of, et(cnt), AX.X, ALU.add))
            thr = con[:, C_THR:C_THR + TILES].unsqueeze(1).to_broadcast([P, EXPERTS, TILES])
            link(dve, dve.tensor_tensor(et(sh), n_of.unsqueeze(2).to_broadcast([P, EXPERTS, TILES]), thr, ALU.is_gt))
            link(dve, dve.tensor_reduce(n_tiles, et(sh), AX.X, ALU.add))
            link(dve, dve.tensor_tensor_scan(upto, ones[:, 0:EXPERTS], n_tiles, 0.0, ALU.mult, ALU.add))
            link(dve, dve.tensor_tensor(before, upto, n_tiles, ALU.subtract))
            link(dve, dve.scalar_tensor_tensor(out=adj, in0=before, scalar=float(P), in1=et(exc)[:, :, 0],
                                               op0=ALU.mult, op1=ALU.subtract))
            link(dve, dve.tensor_tensor(et(inc), et(exc), adj.unsqueeze(2).to_broadcast([P, EXPERTS, TILES]), ALU.add))
            link(dve, dve.tensor_tensor(te(sh), te(bank[3][:, 0:TILES * EXPERTS]),
                                        et(inc).rearrange("p e t -> p t e"), ALU.add))
            link(dve, dve.tensor_tensor(sh, sh, oh, ALU.mult))
            link(dve, dve.tensor_reduce(place_f, te(sh), AX.X, ALU.add))
            link(dve, dve.tensor_copy(place[:, :], place_f))
            le = [P, NG, EXPERTS - 1]
            link(dve, dve.tensor_tensor(first_le[:, :, :], upto[:, 0:EXPERTS - 1].unsqueeze(1).to_broadcast(le),
                                        con[:, C_TIX:C_TIX + NG].unsqueeze(2).to_broadcast(le), ALU.is_le))
            link(dve, dve.tensor_reduce(expert_f[:, :], first_le[:, :, :], AX.X, ALU.add))
            dve.tensor_copy(expert_of[:, :], expert_f[:, :]).then_inc(s.routed, 1)
            dve.wait_ge(s.routed, 1)

            def expert_at(j):
                return dve.value_load(expert_of[0:1, bass.ds(j, 1)], min_val=0, max_val=EXPERTS - 1)

            def relu(j, p):
                e = expert_at(j)
                dve.wait_ge(s.ht_mm, j + 1)
                if not (isinstance(j, int) and j < 2):
                    dve.wait_ge(s.y_mm, j - 1)
                for c in range(FC):
                    ins = dve.tensor_scalar(HT[:, p, c, :], bank[3 + p][:, c * P:(c + 1) * P],
                                            b1_col[:, bass.ds(e * FC + c, 1)], 0.0, ALU.add, ALU.max)
                ins.then_inc(s.ht_out, 1)
                return e

            def add_b2(j, r, e, stores):
                dve.wait_ge(s.y_mm, j + 1)
                if stores is not None:
                    dve.wait_ge(s.y_stored[r], stores * 16)
                dve.tensor_tensor(Y[:, r, :], bank[5 + r % 2][:, 0:D], b2_all[:, bass.ds(e * D, D)],
                                  ALU.add).then_inc(s.y_out, 1)

            for j in range(RING):
                e_now = relu(j, j % 2)
                if j >= 1:
                    add_b2(j - 1, j - 1, e_last, None)
                e_last = e_now
            with dve.Fori(1, NG // RING) as q:
                for r in range(RING):
                    if r == 0:
                        e_last = expert_at(q * RING - 1)
                    e_now = relu(q * RING + r, r % 2)
                    add_b2(q * RING + (r - 1), (r - 1) % RING, e_last, q if r else q - 1)
                    e_last = e_now
            add_b2(NG - 1, RING - 1, expert_at(NG - 1), NG // RING - 1)

            for g in range(TILES // ROW):
                dve.wait_ge(s.gathered[g], 16 * ROW)
                for t in range(g * ROW, (g + 1) * ROW):
                    ins = dve.scalar_tensor_tensor(out=X[:, t, :], in0=XN[:, t, :], scalar=half_gate[:, t:t + 1],
                                                   in1=X[:, t, :], op0=ALU.mult, op1=ALU.add)
                ins.then_inc(s.added, 1)

        def ffn_gpsimd(pool, s, n):
            pool.wait_ge(s.routed, 1)
            if n == 0:
                pool.wait_ge(zero_fill, 16)
            for t in range(TILES):
                pool.indirect_dma_start(out=grouped_x, out_offset=bass.IndirectOffsetOnAxis(ap=place[:, t:t + 1], axis=0),
                                        in_=XN[:, t, :], in_offset=None).then_inc(s.scattered, 16)
            if n == 0:
                pool.wait_ge(attn_w_in, 16 * 7)
                pool.tensor_copy(w_hi[:, :, :], w_raw[:, :, :]).then_inc(w_hi_set, 1)
                pool.wait_ge(w_hi_set, 1)
                pool.tensor_tensor(w_lo[:, :, :], w_raw[:, :, :], w_hi[:, :, :].bitcast(F32),
                                   ALU.subtract).then_inc(w_lo_set, 1)
            for r in range(RING):
                pool.wait_ge(s.y_stored[r], 16 * (NG // RING))
            pool.wait_ge(s.scattered, 16 * TILES)
            for t in range(TILES):
                pool.indirect_dma_start(out=XN[:, t, :], out_offset=None, in_=grouped_y,
                                        in_offset=bass.IndirectOffsetOnAxis(ap=place[:, t:t + 1], axis=0)
                                        ).then_inc(s.gathered[t // ROW], 16)

        WO_BANK, TX_BANK = 6, 0
        V_AT = ((4, 5), (6, 7))
        PROB_LAG, TURN_LAG, PV_LAG = 2, 3, 4

        def behind(b, h, lag):
            return (b - 1, h - lag + HEADS) if h < lag else (b, h - lag)

        def pe_turn_x(pe, b, first=False):
            pe.wait_ge(xn_set, b + 1)
            if not first:
                pe.wait_ge(v_set, 4 * b - 1)
            for t in range(QT):
                mm = pe.transpose(bank[TX_BANK][:, t * P:(t + 1) * P], xn[:, t, :], ident)
            mm.then_inc(xT_mm, 1)

        def pe_project(pe, tau, half, m):
            kind, t = m // QT, m % QT
            bk = m % 2
            n = tau if isinstance(tau, int) else tau[0]
            if m == 0:
                pe.wait_ge(xT_lo_set, (tau - half) // 2 + 1 if isinstance(tau, int) else tau[1] + 1)
                if half == 1:
                    pe.wait_ge(v_set, 2 * n - 1)
            elif m == 1:
                if not (isinstance(n, int) and n == 0):
                    pe.wait_ge(v_set, 2 * n)
            else:
                pe.wait_ge(rope_w, 4 * n + m - 1)
            for a, (xs, ws) in enumerate(((xT_hi, w_hi), (xT_hi, w_lo), (xT_lo, w_hi))):
                mm = pe.matmul(bank[bk][:, :], xs[:, t * P:(t + 1) * P], ws[:, 2 * kind + half, :],
                               start=(a == 0), stop=(a == 2))
            mm.then_inc(proj_mm, 1)

        def pe_turn_qk(pe, n, half, j, wo_before=None):
            if j == 0:
                pe.wait_ge(rot_set, 4 * n + 4)
            if not (isinstance(n, int) and n == 0 and j == 0):
                pe.wait_ge(qk_lo_set, 4 * n + j)
            if wo_before is not None:
                pe.wait_ge(wo_added, wo_before)
            for kind in range(2):
                for t in range(QT):
                    mm = pe.transpose(bank[6][:, (kind * QT + t) * P:(kind * QT + t + 1) * P],
                                      rot[:, kind, t, j * P:(j + 1) * P], ident)
            mm.then_inc(turn_mm, 1)

        def pe_scores(pe, b, h, first=False):
            half, i = h // HALF, h % HALF
            j, at = i // 2, HEAD * (i % 2)
            if i % 2 == 0:
                pe.wait_ge(qk_lo_set, 8 * b + 4 * half + j + 1)
            if not first:
                pe.wait_ge(exp_set, HEADS * b + h - 1)
            q = [a[at:at + HEAD, half, j, 0, :] for a in (qk_hi, qk_lo)]
            k = [a[at:at + HEAD, half, j, 1, :] for a in (qk_hi, qk_lo)]
            for t in range(QT):
                for a, (x1, x2) in enumerate(((0, 0), (0, 1), (1, 0))):
                    mm = pe.matmul(bank[2 + h % 2][:, t * SEQ:(t + 1) * SEQ], q[x1][:, t * P:(t + 1) * P], k[x2],
                                   start=(a == 0), stop=(a == 2))
            mm.then_inc(score_mm, 1)

        def pe_turn_e(pe, b, h, first=False):
            pe.wait_ge(prob_set, HEADS * b + h + 1)
            if not first:
                pe.wait_ge(et_set, HEADS * b + h - 1)
            for kt in range(QT):
                for t in range(QT):
                    mm = pe.transpose(bank[4 + h % 2][:, kt * SEQ + t * P:kt * SEQ + (t + 1) * P],
                                      E[:, h % 4, t, kt * P:(kt + 1) * P], ident)
            mm.then_inc(et_mm, 1)

        def pe_pv(pe, b, h, first=False):
            half, i = h % HEADS // HALF, h % HALF
            at = HEAD * (i % 2)
            pe.wait_ge(et_set, HEADS * b + h + 1)
            if i == 0:
                pe.wait_ge(v_set, 4 * b + 2 * half + 2)
            if i % 2 == 0 and not first:
                pe.wait_ge(ot_set, 8 * b + h // 2)
            for kt in range(QT):
                mm = pe.matmul(bank[7][at:at + HEAD, 0:SEQ], V[:, half, kt, i * HEAD:(i + 1) * HEAD],
                               ET[:, h % 2, kt * SEQ:(kt + 1) * SEQ], start=(kt == 0), stop=(kt == QT - 1))
            mm.then_inc(pv_mm, 1)

        def pe_wo(pe, b, b_prev, last=False):
            pe.wait_ge(ot_set, 8 * (b_prev + 1))
            if not last:
                pe.wait_ge(qk_lo_set, 8 * b + 4)
            for t in range(QT):
                for j in range(HEADS // 2):
                    mm = pe.matmul(bank[WO_BANK][:, t * D:(t + 1) * D], OT[:, j, t * P:(t + 1) * P], Wo[:, j, :],
                                   start=(j == 0), stop=(j == HEADS // 2 - 1))
            mm.then_inc(wo_mm, 1)

        def pe_batch(pe, b, first=False, last=False):
            for half in range(2):
                prep = not (last and half == 1)
                tau = 2 * b + half + 1
                tgt = 1 - half
                tb = (tau, b + half)
                for i in range(HALF):
                    h = HALF * half + i
                    pe_scores(pe, b, h, first=first and h < 2)
                    if not (first and h < TURN_LAG):
                        pe_turn_e(pe, *behind(b, h, TURN_LAG), first=first and h - TURN_LAG < 2)
                    if i == 1:
                        pe_turn_qk(pe, 2 * b + half, half, 3)
                    if prep and (i < 4 or i in V_AT[half]):
                        pe_project(pe, tb, tgt, i if i < 4 else 4 + V_AT[half].index(i))
                    if not (first and h < PV_LAG):
                        pe_pv(pe, *behind(b, h, PV_LAG), first=first and h - PV_LAG < 2)
                    if half == 0 and i == 4 and not first:
                        pe_wo(pe, b, b - 1)
                    if half == 0 and i == 6 and not last:
                        pe_turn_x(pe, b + 1)
                    if prep and i >= 5:
                        pe_turn_qk(pe, tau, tgt, i - 5, wo_before=b if i == 5 and half == 0 and not first else None)

        def attention_tensor(pe):
            pe.wait_ge(w_lo_set, 1)
            pe_turn_x(pe, 0, first=True)
            for m in range(6):
                pe_project(pe, 0, 0, m)
            for j in range(PAIRS - 1):
                pe_turn_qk(pe, 0, 0, j)
            pe_batch(pe, 0, first=True)
            with pe.Fori(1, BATCH - 1) as b:
                pe_batch(pe, b)
            pe_batch(pe, BATCH - 1, last=True)
            for h in range(HEADS, HEADS + PV_LAG):
                if h - TURN_LAG < HEADS:
                    pe_turn_e(pe, BATCH - 1, h - TURN_LAG)
                pe_pv(pe, BATCH - 1, h - PV_LAG)
            pe_wo(pe, BATCH, BATCH - 1, last=True)

        def act_hi(act, n, half, j):
            act.wait_ge(turn_mm, 4 * n + j + 1)
            act.activation(qk_hi[:, half, j, :, :], bank[6][:, :].rearrange("p (k s) -> p k s", k=2),
                           ACT.Copy).then_inc(qk_hi_set, 1)

        def act_v(act, n, half, t):
            act.wait_ge(proj_mm, 6 * n + 5 + t)
            act.activation(V[:, half, t, :], bank[t % 2][:, :], ACT.Copy).then_inc(v_set, 1)

        def act_x_hi(act, b):
            act.wait_ge(xT_mm, b + 1)
            act.activation(xT_hi[:, :], bank[TX_BANK][:, 0:SEQ], ACT.Copy).then_inc(xT_hi_set, 1)

        def act_ot(act, b, j, first=False):
            act.wait_ge(pv_mm, HEADS * b + 2 * j + 2)
            if not first:
                act.wait_ge(wo_mm, b)
            act.activation(OT[:, j, :], bank[7][:, 0:SEQ], ACT.Copy).then_inc(ot_set, 1)

        def act_et(act, b, h, first=False):
            act.wait_ge(et_mm, HEADS * b + h + 1)
            if not first:
                act.wait_ge(pv_mm, HEADS * b + h - 1)
            act.activation(ET[:, h % 2, :], bank[4 + h % 2][:, :], ACT.Copy).then_inc(et_set, 1)

        def act_exp(act, b, h, first=False):
            act.wait_ge(max_set, HEADS * b + h + 1)
            if not first:
                act.wait_ge(et_mm, HEADS * b + h - 3)
            for t in range(QT):
                ins = act.activation(E[:, h % 4, t, :], bank[2 + h % 2][:, t * SEQ:(t + 1) * SEQ], ACT.Exp,
                                     bias=negmax[:, h % 2, t:t + 1], accum_out=total[:, h % 2, t:t + 1])
            ins.then_inc(exp_set, 1)

        def act_batch(act, b, first=False, last=False):
            for half in range(2):
                prep = not (last and half == 1)
                tau = 2 * b + half + 1
                tgt = 1 - half
                for i in range(HALF):
                    h = HALF * half + i
                    if i == 0 or i == 3:
                        act_hi(act, 2 * b + half, half, 2 if i == 0 else 3)
                    if prep and i >= 6:
                        act_hi(act, tau, tgt, i - 6)
                    if h % 2 == 0 and not (first and h < PV_LAG + 2):
                        eb, eh = behind(b, h, PV_LAG + 2)
                        act_ot(act, eb, eh // 2, first=first)
                    if not (first and h < 1):
                        act_exp(act, *behind(b, h, 1), first=first and h < 5)
                    if not (first and h < TURN_LAG):
                        act_et(act, *behind(b, h, TURN_LAG), first=first and h - TURN_LAG < 2)
                    if prep and i in V_AT[half]:
                        act_v(act, tau, tgt, V_AT[half].index(i))
                    if half == 0 and i == 6 and not last:
                        act_x_hi(act, b + 1)

        def attention_scalar(act):
            act.wait_ge(ln2_var, 1)
            act.activation(ln[:, 1, :], ln[:, 0, :], ACT.Sqrt).then_inc(ln2_sqrt, 1)
            act_x_hi(act, 0)
            for t in range(QT):
                act_v(act, 0, 0, t)
            for j in range(PAIRS - 2):
                act_hi(act, 0, 0, j)
            act_batch(act, 0, first=True)
            with act.Fori(1, BATCH - 1) as b:
                act_batch(act, b)
            act_batch(act, BATCH - 1, last=True)
            for h in range(HEADS, HEADS + PV_LAG + 1):
                if h == HEADS:
                    act_exp(act, BATCH - 1, HEADS - 1)
                if h % 2 == 0:
                    act_ot(act, BATCH - 1, (h - PV_LAG - 2) // 2)
                if h - TURN_LAG < HEADS:
                    act_et(act, BATCH - 1, h - TURN_LAG)

        def dve_xn(dve, b, first=False):
            if not first:
                dve.wait_ge(xT_mm, b)
            for t in range(QT):
                tile = b * QT + t
                ins = dve.tensor_scalar(xn[:, t, :], X[:, bass.ds(tile, 1), :].squeeze(1) if not isinstance(b, int) else X[:, tile, :],
                                        mv[:, bass.ds(tile, 1), 0:1].squeeze(1), rstd[:, bass.ds(tile, 1)],
                                        ALU.subtract, ALU.mult)
            ins.then_inc(xn_set, 1)

        def dve_x_lo(dve, b):
            dve.wait_ge(xT_hi_set, b + 1)
            dve.tensor_tensor(xT_lo[:, :], bank[TX_BANK][:, 0:SEQ], xT_hi[:, :].bitcast(F32),
                              ALU.subtract).then_inc(xT_lo_set, 1)

        def dve_rope(dve, n, half, m, first=False):
            kind, t = m // QT, m % QT
            dve.wait_ge(proj_mm, 6 * n + m + 1)
            if not (first and m < 2):
                dve.wait_ge(rot_set, 4 * n + m - 1)
            src = bank[m % 2][:, :]
            pb = m % 2
            dve.tensor_tensor(rot_u[:, pb, :].rearrange("p (h d) -> p h d", d=HEAD),
                              src.rearrange("p (h d) -> p h d", d=HEAD),
                              table(kind, 0, t).unsqueeze(1).to_broadcast([P, HALF, HEAD]), ALU.mult)
            dve.tensor_tensor(rot_w[:, pb, :].rearrange("p (h j d) -> p h j d", j=2, h=HALF)[:, :, ::-1, :],
                              src.rearrange("p (h j d) -> p h j d", j=2, h=HALF),
                              table(kind, 1, t).rearrange("p (j d) -> p j d", j=2).unsqueeze(1)
                              .to_broadcast([P, HALF, 2, HEAD // 2]), ALU.mult).then_inc(rope_w, 1)

        def dve_lo(dve, n, half, j):
            dve.wait_ge(qk_hi_set, 4 * n + j + 1)
            dve.tensor_tensor(qk_lo[:, half, j, :, :], bank[6][:, :].rearrange("p (k s) -> p k s", k=2),
                              qk_hi[:, half, j, :, :].bitcast(F32), ALU.subtract).then_inc(qk_lo_set, 1)

        def dve_max(dve, b, h):
            dve.wait_ge(score_mm, HEADS * b + h + 1)
            dve.tensor_reduce(negmax[:, h % 2, :], bank[2 + h % 2][:, :].rearrange("p (t s) -> p t s", t=QT),
                              AX.X, ALU.max, negate=True).then_inc(max_set, 1)

        def dve_prob(dve, b, h):
            dve.wait_ge(exp_set, HEADS * b + h + 1)
            dve.reciprocal(recip[:, h % 2, :], total[:, h % 2, :]).then_inc(recip_set, 1)
            dve.wait_ge(recip_set, HEADS * b + h + 1)
            for t in range(QT):
                ins = dve.tensor_scalar(E[:, h % 4, t, :], E[:, h % 4, t, :], recip[:, h % 2, t:t + 1], None, ALU.mult)
            ins.then_inc(prob_set, 1)

        def dve_wo(dve, b):
            dve.wait_ge(wo_mm, b + 1)
            xs = X[:, bass.ds(b * QT, QT), :]
            dve.tensor_tensor(xs, bank[WO_BANK][:, 0:QT * D].rearrange("p (t d) -> p t d", t=QT), xs,
                              ALU.add).then_inc(wo_added, 1)

        def dve_batch(dve, b, first=False, last=False):
            for half in range(2):
                prep = not (last and half == 1)
                tau = 2 * b + half + 1
                tgt = 1 - half
                for i in range(HALF):
                    h = HALF * half + i
                    if i == 0 or i == 4:
                        dve_lo(dve, 2 * b + half, half, 2 if i == 0 else 3)
                    if prep and i >= 6:
                        dve_lo(dve, tau, tgt, i - 6)
                    if not (first and h < PROB_LAG):
                        dve_prob(dve, *behind(b, h, PROB_LAG))
                    dve_max(dve, b, h)
                    if half == 0 and i == 5 and not first:
                        dve_wo(dve, b - 1)
                    if half == 0 and i == 4 and not last:
                        dve_xn(dve, b + 1)
                    if prep and i < 4:
                        dve_rope(dve, tau, tgt, i)
                    if half == 0 and i == 6 and not last:
                        dve_x_lo(dve, b + 1)

        def attention_vector(dve):
            for t in range(TILES):
                ins = dve.bn_stats(stats[:, t, :], X[:, t, :])
            link(dve, ins)
            aggregate(dve)
            norm_stats(dve, ln2_var, ln2_sqrt)
            dve_xn(dve, 0, first=True)
            dve_x_lo(dve, 0)
            for m in range(4):
                dve_rope(dve, 0, 0, m, first=True)
            for j in range(PAIRS - 2):
                dve_lo(dve, 0, 0, j)
            dve_batch(dve, 0, first=True)
            with dve.Fori(1, BATCH - 1) as b:
                dve_batch(dve, b)
            dve_batch(dve, BATCH - 1, last=True)
            for h in range(HEADS - PROB_LAG, HEADS):
                dve_prob(dve, BATCH - 1, h)
            dve_wo(dve, BATCH - 1)
            dve.wait_ge(wo_added, BATCH)

        def pool_rot(pool, n, m):
            pool.wait_ge(rope_w, 4 * n + m + 1)
            if m == 0 and not (isinstance(n, int) and n == 0):
                pool.wait_ge(turn_mm, 4 * n)
            pool.tensor_tensor(rot[:, m // QT, m % QT, :], rot_u[:, m % 2, :], rot_w[:, m % 2, :],
                               ALU.add).then_inc(rot_set, 1)

        def attention_gpsimd(pool):
            pool.wait_ge(ffn[0].added, TILES // ROW)
            for m in range(4):
                pool_rot(pool, 0, m)
            with pool.Fori(1, 2 * BATCH) as n:
                for m in range(4):
                    pool_rot(pool, n, m)

        @block.sync
        def _(sp):
            sp.dma_start(con[:, :], consts).then_inc(con_in, 16)
            for g in range(4):
                sp.dma_start(X[:, 8 * g:8 * g + 8, :], x_t[:, 8 * g:8 * g + 8, :]).then_inc(x_in[g], 16)
            sp.dma_start(Wr[:, :], wr).then_inc(small_in, 16)
            sp.dma_start(br_all[:, :], br.rearrange("(a e) -> a e", a=1).to_broadcast([P, EXPERTS])).then_inc(small_in, 16)
            sp.dma_start(b1_rows[:, :], b1.rearrange("e (c p) -> (e c) p", p=P)).then_inc(small_in, 16)
            sp.dma_start(b2_all[:, :], b2.rearrange("(a e) d -> a (e d)", a=1).to_broadcast([P, EXPERTS * D])
                         ).then_inc(small_in, 16)
            sp.wait_ge(const_set, 1)
            sp.dma_start(grouped_x.rearrange("(n p) d -> p n d", p=P),
                         zero[:, :].unsqueeze(1).to_broadcast([P, NG, D])).then_inc(zero_fill, 16)
            sp.dma_start(W1[:, :].rearrange("p (e f) -> p e f", e=EXPERTS), w1.rearrange("e p f -> p e f")
                         ).then_inc(ffn_w_in, 16)
            sp.dma_start(W2[:, :].rearrange("p (e c d) -> p e c d", e=EXPERTS, c=FC),
                         w2.rearrange("e (c p) d -> p e c d", p=P)).then_inc(ffn_w_in, 16)
            for k, w in enumerate((wq, wk, wv)):
                for half in range(2):
                    sp.dma_start(w_raw[:, 2 * k + half, :], w[:, 512 * half:512 * half + 512]).then_inc(attn_w_in, 16)
            sp.dma_start(Wo[:, :, :], wo.rearrange("(j p) d -> p j d", p=P)).then_inc(attn_w_in, 16)
            ffn_load_store(sp, ffn[0])
            ffn_load_store(sp, ffn[1])
            for g in range(TILES // ROW):
                sp.wait_ge(ffn[1].added, g + 1)
                sp.dma_start(out_t[:, ROW * g:ROW * g + ROW, :], X[:, ROW * g:ROW * g + ROW, :]).then_inc(out_done, 16)
            sp.wait_ge(out_done, 16 * (TILES // ROW))

        @block.tensor
        def _(pe):
            pe.wait_ge(con_in, 16)
            ffn_tensor(pe, ffn[0], 0)
            attention_tensor(pe)
            ffn_tensor(pe, ffn[1], 1)

        @block.scalar
        def _(act):
            ffn_scalar(act, ffn[0])
            attention_scalar(act)
            ffn_scalar(act, ffn[1])

        @block.vector
        def _(dve):
            dve.memset(zero[:, :], 0.0).then_inc(const_set, 1)
            dve.memset(ones[:, :], 1.0).then_inc(const_set, 1)
            ffn_vector(dve, ffn[0], 0)
            dve.wait_ge(ffn[0].added, TILES // ROW)
            attention_vector(dve)
            ffn_vector(dve, ffn[1], 1)

        @block.gpsimd
        def _(pool):
            ffn_gpsimd(pool, ffn[0], 0)
            attention_gpsimd(pool)
            ffn_gpsimd(pool, ffn[1], 1)


def even_odd(w):
    return w.reshape(D, HEADS, HEAD // 2, 2).transpose(0, 1, 3, 2).reshape(D, HEADS * HEAD)


def kernel(L0_attn_x, L0_attn_Wq, L0_attn_Wk, L0_attn_Wv, L0_attn_Wo, L0_ffn_Wr, L0_ffn_br, L0_ffn_W1, L0_ffn_b1,
           L0_ffn_W2, L0_ffn_b2):
    import numpy as np
    import concourse.bacc as bacc
    from concourse.bass_utils import run_bass_kernel_spmd

    arrays = {
        "x": np.asarray(L0_attn_x), "wq": even_odd(np.asarray(L0_attn_Wq)), "wk": even_odd(np.asarray(L0_attn_Wk)),
        "wv": np.asarray(L0_attn_Wv), "wo": np.asarray(L0_attn_Wo), "wr": np.asarray(L0_ffn_Wr),
        "br": np.asarray(L0_ffn_br), "w1": np.asarray(L0_ffn_W1), "b1": np.asarray(L0_ffn_b1),
        "w2": np.asarray(L0_ffn_W2), "b2": np.asarray(L0_ffn_b2), "consts": constants(),
    }
    arrays = {f"in_{name}": np.ascontiguousarray(a) for name, a in arrays.items()}
    nc = bacc.Bacc("TRN2", target_bir_lowering=False, num_devices=1)
    args = [nc.dram_tensor(name, a.shape, mybir.dt.from_np(a.dtype), kind="ExternalInput").ap()
            for name, a in arrays.items()]
    out = nc.dram_tensor("out_0", (BATCH, SEQ, D), F32, kind="ExternalOutput").ap()
    macaron_kernel(nc, *args, out)
    r = run_bass_kernel_spmd(nc, [arrays], core_ids=[0])
    return r.results[0]["out_0"]
```

```python
from contextlib import ExitStack

import concourse.bass as bass
from concourse import mybir

F32 = mybir.dt.float32
F32R = mybir.dt.float32r
I32 = mybir.dt.int32
U32 = mybir.dt.uint32
ALU = mybir.AluOpType
ACT = mybir.ActivationFunctionType
AX = mybir.AxisListType

P = 128
BATCH, SEQ, D = 16, 256, 128
HEADS, HEAD = 16, 64
EXPERTS, DFF = 8, 512
TILES = BATCH * SEQ // P
QT = SEQ // P
PARTS = 2
PT = TILES // PARTS
NGP = PT + EXPERTS
NG = PARTS * NGP
FC = DFF // P
HALF = HEADS // 2
PAIRS = HALF // 2
EPS = 1e-5
ROW = 4
RING = 4

C_ID, C_LOW, C_ONE = 0, P, 2 * P
C_ROPE = 3 * P
C_DESC = C_ROPE + 4 * QT * HEAD
C_THR = C_DESC + EXPERTS
C_TIX = C_THR + PT
C_TOKEN = C_TIX + NGP
C_ALL = C_TOKEN + PT + NGP


def constants():
    import numpy as np

    f = np.float32
    c = np.zeros((P, C_ALL), f)
    c[:, C_ID:C_ID + P] = np.eye(P, dtype=f)
    c[:, C_LOW:C_LOW + P] = np.triu(np.ones((P, P), f), 1)
    c[:, C_ONE:C_ONE + P] = 1
    pos = np.arange(SEQ, dtype=f)
    i = np.arange(HEAD // 2, dtype=f)
    cos, sin = [], []
    for s in (1.0, 4.0, 16.0):
        freq = f(1.0) / np.power(f(10000.0 * s), f(2.0) * i / f(HEAD), dtype=f)
        ang = pos[:, None] * freq[None, :]
        cos.append(np.cos(ang))
        sin.append(np.sin(ang))
    cos = np.mean(np.stack(cos), 0, dtype=f)
    sin = np.mean(np.stack(sin), 0, dtype=f)
    scale = f(HEAD) ** f(-0.5)
    for n, (a, b) in enumerate(((cos, cos), (sin, -sin))):
        t = np.concatenate([a, b], 1).reshape(QT, P, HEAD).transpose(1, 0, 2).reshape(P, QT * HEAD)
        at = C_ROPE + n * QT * HEAD
        c[:, at:at + QT * HEAD] = t * scale
        c[:, at + 2 * QT * HEAD:at + 3 * QT * HEAD] = t
    c[:, C_DESC:C_DESC + EXPERTS] = np.arange(EXPERTS, 0, -1)
    c[:, C_THR:C_THR + PT] = P * np.arange(PT)
    c[:, C_TIX:C_TIX + NGP] = np.arange(NGP)
    c[:, C_TOKEN:C_TOKEN + PT + NGP] = P * np.arange(PT + NGP)[None, :] + np.arange(P)[:, None]
    return c


def macaron_kernel(nc, x, wq, wk, wv, wo, wr, br, w1, b1, w2, b2, consts, out):
    x_t = x.rearrange("b (n p) d -> p (b n) d", p=P)
    out_t = out.rearrange("b (n p) d -> p (b n) d", p=P)
    WIDTH = (D, D + 1)
    grouped_x = [nc.dram_tensor(f"grouped_x{k}", [NGP * P, WIDTH[k]], F32).ap() for k in range(PARTS)]
    results = nc.dram_tensor("results", [(PT + NGP) * P, D], F32).ap()
    grouped_y = [nc.dram_tensor(f"grouped_y{k}", [NGP * P, D], F32).ap() for k in range(PARTS)]

    with ExitStack() as ctx:
        def sb(name, shape, dt=F32):
            return ctx.enter_context(nc.sbuf_tensor(name, shape, dt))

        def sem(name):
            return ctx.enter_context(nc.semaphore(name))

        bank = [ctx.enter_context(nc.psum_tensor(f"bank{n}", [P, 512], F32)) for n in range(8)]

        con = sb("con", [P, C_ALL])
        X = sb("X", [P, TILES, D])
        XN = sb("XN", [P, TILES, D + 1])
        W1_hi = sb("W1_hi", [P, EXPERTS * DFF], F32R)
        W2 = sb("W2", [P, EXPERTS * FC * D])
        b1_rows = sb("b1_rows", [EXPERTS * FC, P])
        b1_col = sb("b1_col", [P, EXPERTS * FC])
        b2_all = sb("b2_all", [P, EXPERTS * D])
        Wr = sb("Wr", [P, EXPERTS])
        br_all = sb("br_all", [P, EXPERTS])
        blank = sb("blank", [P, D + 1])
        ones = sb("ones", [P, PT * EXPERTS])
        w_raw = sb("w_raw", [P, 6, 512])
        w_hi = sb("w_hi", [P, 6, 512], F32R)
        w_lo = sb("w_lo", [P, 6, 512], F32R)
        Wo = sb("Wo", [P, HEADS // 2, D])
        stats = sb("stats", [P, TILES, 6])
        mv = sb("mv", [P, TILES, 2])
        ln = sb("ln", [P, 6, TILES])
        rstd = ln[:, 5, :]
        XNT = sb("XNT", [P, 2, ROW * P])
        R = sb("R", [P, 8, TILES * EXPERTS])
        small = sb("small", [P, 12, TILES])
        expert_f = sb("expert_f", [P, NG])
        expert_of = sb("expert_of", [P, NG], I32)
        place = sb("place", [P, TILES], U32)
        half_gate = sb("half_gate", [P, TILES])
        XG = sb("XG", [P, RING, D + 1])
        token = sb("token", [P, NGP + 1], U32)
        XT_hi = sb("XT_hi", [P, 2, P], F32R)
        XT_lo = sb("XT_lo", [P, 2, P], F32R)
        shared = sb("shared", [P, 4 * DFF])
        Hs = shared[:, 0:2 * DFF].rearrange("p (r f) -> p r f", r=2)
        HT = shared[:, 2 * DFF:4 * DFF].rearrange("p (r c t) -> p r c t", r=2, c=FC)
        Y = sb("Y", [P, RING, D])
        first_le = Y[:, :, :].rearrange("p r d -> p (r d)")[:, 0:PARTS * NGP * (EXPERTS - 1)].rearrange(
            "p (k n e) -> p k n e", k=PARTS, e=EXPERTS - 1)
        xn = sb("xn", [P, QT, D])
        xT_hi = sb("xT_hi", [P, SEQ], F32R)
        xT_lo = sb("xT_lo", [P, SEQ], F32R)
        rot_u = sb("rot_u", [P, 2, 512])
        rot_w = sb("rot_w", [P, 2, 512])
        rot = w_raw[:, 0:2 * QT, :].rearrange("p (k t) c -> p k t c", k=2)
        qk_hi = sb("qk_hi", [P, 2, PAIRS, 2, SEQ], F32R)
        qk_lo = sb("qk_lo", [P, 2, PAIRS, 2, SEQ], F32R)
        W1_lo = qk_hi[:, :, :, :, :].rearrange("p h j k s -> p (h j k s)")
        V = sb("V", [P, 2, QT, 512])
        negmax = sb("negmax", [P, 2, QT])
        total = sb("total", [P, 2, QT])
        recip = sb("recip", [P, 2, QT])
        E = sb("E", [P, 4, QT, SEQ])
        W1_raw = (E[:, :, :, :].rearrange("p r t s -> p (r t s)"), V[:, :, :, :].rearrange("p h t s -> p (h t s)"))
        W1_HALF = EXPERTS * DFF // 2
        ET = sb("ET", [P, 2, QT * SEQ])
        OT = shared[:, :].rearrange("p (j s) -> p j s", j=HEADS // 2)

        ident = con[:, C_ID:C_ID + P]
        lower = con[:, C_LOW:C_LOW + P]
        ones_sq = con[:, C_ONE:C_ONE + P]

        def table(kind, which, tt):
            at = C_ROPE + ((2 * kind + which) * QT + tt) * HEAD
            return con[:, at:at + HEAD]

        x_in = [sem(f"x_in{n}") for n in range(4)]
        con_in = sem("con_in")
        small_in = sem("small_in")
        ffn_w_in = sem("ffn_w_in")
        attn_w_in = sem("attn_w_in")
        const_set = sem("const_set")
        zero_fill = sem("zero_fill")
        w1_in = sem("w1_in")
        w1_hi_set = sem("w1_hi_set")
        w1_lo_set = sem("w1_lo_set")
        w_hi_set = sem("w_hi_set")
        w_lo_set = sem("w_lo_set")
        b1_turned = sem("b1_turned")
        b1_set = sem("b1_set")
        dve_step = sem("dve_step")
        out_done = sem("out_done")
        steps = [0]

        def link(eng, ins):
            ins.then_inc(dve_step, 1)
            steps[0] += 1
            eng.wait_ge(dve_step, steps[0])

        class Sems:
            pass

        def ffn_sems(n):
            s = Sems()
            s.var_ready = sem(f"f{n}_var_ready")
            s.sqrt_ready = sem(f"f{n}_sqrt_ready")
            s.normed = sem(f"f{n}_normed")
            s.turned = sem(f"f{n}_turned")
            s.turned_out = sem(f"f{n}_turned_out")
            s.logits = sem(f"f{n}_logits")
            s.shifted = sem(f"f{n}_shifted")
            s.exped = sem(f"f{n}_exped")
            s.onehot = sem(f"f{n}_onehot")
            s.ranked = sem(f"f{n}_ranked")
            s.placed = sem(f"f{n}_placed")
            s.routed = sem(f"f{n}_routed")
            s.scattered = [sem(f"f{n}_scattered{k}") for k in range(PARTS)]
            s.xg_in = [sem(f"f{n}_xg_in{r}") for r in range(RING)]
            s.xt_mm = sem(f"f{n}_xt_mm")
            s.xt_hi_out = sem(f"f{n}_xt_hi_out")
            s.xt_lo_out = sem(f"f{n}_xt_lo_out")
            s.h_mm = sem(f"f{n}_h_mm")
            s.h_out = sem(f"f{n}_h_out")
            s.ht_mm = sem(f"f{n}_ht_mm")
            s.ht_out = sem(f"f{n}_ht_out")
            s.y_mm = sem(f"f{n}_y_mm")
            s.y_out = sem(f"f{n}_y_out")
            s.y_stored = [sem(f"f{n}_y_stored{r}") for r in range(RING)]
            s.gathered = [sem(f"f{n}_gathered{r}") for r in range(TILES // ROW)]
            s.added = sem(f"f{n}_added")
            s.token_set = sem(f"f{n}_token_set")
            s.y_sent = [sem(f"f{n}_y_sent{r}") for r in range(RING)]
            s.measured = sem(f"f{n}_measured")
            return s

        ffn = [ffn_sems(0), ffn_sems(1)]

        ln2_var = sem("ln2_var")
        ln2_sqrt = sem("ln2_sqrt")
        xn_set = sem("xn_set")
        xT_mm = sem("xT_mm")
        xT_hi_set = sem("xT_hi_set")
        xT_lo_set = sem("xT_lo_set")
        proj_mm = sem("proj_mm")
        rope_w = sem("rope_w")
        rot_set = sem("rot_set")
        v_set = sem("v_set")
        turn_mm = sem("turn_mm")
        qk_hi_set = sem("qk_hi_set")
        qk_lo_set = sem("qk_lo_set")
        score_mm = sem("score_mm")
        max_set = sem("max_set")
        exp_set = sem("exp_set")
        recip_set = sem("recip_set")
        prob_set = sem("prob_set")
        prob_act_set = sem("prob_act_set")
        et_mm = sem("et_mm")
        et_set = sem("et_set")
        pv_mm = sem("pv_mm")
        ot_set = sem("ot_set")
        wo_mm = sem("wo_mm")
        wo_added = sem("wo_added")

        block = ctx.enter_context(nc.Block())

        LOGIT_BANK, X_BANK = 6, (0, 7)
        AHEAD = 5

        def ffn_load_store(sp, s, n):
            def load(part, j, r, free):
                if n == 1 and part == 1 and not (isinstance(j, int) and j < NGP + RING - 1):
                    sp.wait_ge(s.token_set, free - (NGP - 1))
                elif free is not None:
                    sp.wait_ge(s.xt_mm, free)
                sp.dma_start(XG[:, r, 0:WIDTH[part]], grouped_x[part][bass.ds((j - part * NGP) * P, P), :]
                             ).then_inc(s.xg_in[r], 16)

            def store(part, j, r):
                if n == 1 and part == 1:
                    return
                sp.wait_ge(s.y_out, j + 1)
                sp.dma_start(grouped_y[part][bass.ds((j - part * NGP) * P, P), :], Y[:, r, :]).then_inc(s.y_stored[r], 16)

            behind = 2 * RING
            for part in range(PARTS):
                sp.wait_ge(s.scattered[part], 16 * PT)
                for j in range(part * NGP, part * NGP + behind):
                    load(part, j, j % RING, j - RING + 1 if j >= RING else None)
                    if part == 1:
                        store(0, j - behind, j % RING)
                first = part * NGP // RING
                with sp.Fori(first + behind // RING, first + NGP // RING) as q:
                    for r in range(RING):
                        load(part, q * RING + r, r, q * RING + (r - RING + 1))
                        store(part, q * RING + (r - behind), r)
            for j in range(NG - behind, NG):
                store(PARTS - 1, j, j % RING)

        def ffn_tensor(pe, s, n):
            for part in range(PARTS):
                if part == 0 and n == 1:
                    continue
                for g in range(part * PT // ROW, (part + 1) * PT // ROW):
                    turn_rows(pe, s, g)
                    if g == 0:
                        pe.wait_ge(small_in, 16 * 4)
                        pe.transpose(bank[5][:, 0:EXPERTS * FC], b1_rows[:, :],
                                     con[0:EXPERTS * FC, C_ID:C_ID + EXPERTS * FC]).then_inc(b1_turned, 1)
                    if g > part * PT // ROW:
                        logits(pe, s, g - 1)
                logits(pe, s, (part + 1) * PT // ROW - 1)
                rank(pe, s, part)

            def turn_x(j, r, q):
                pe.wait_ge(s.xg_in[r], (q + 1) * 16)
                if not (isinstance(j, int) and j < 2):
                    pe.wait_ge(s.xt_lo_out, j - 1)
                pe.transpose(bank[X_BANK[r % 2]][:, 0:P], XG[:, r, 0:D], ident).then_inc(s.xt_mm, 1)

            experts = [pe.alloc_register(f"f{n}_expert{r}") for r in range(RING)]

            def load_expert(q, r):
                pe.reg_load(experts[r % RING], expert_of[0:1, bass.ds(q * RING + r, 1)])

            def expert(r):
                return pe.snap(experts[r % RING], min_val=0, max_val=EXPERTS - 1)

            def slot(q, r, w1=True, th=True, tx=True, w2=True, ahead=True):
                j, p = q * RING + r, r % 2
                if w1:
                    e = expert(r)
                    pe.wait_ge(s.xt_lo_out, j + 1)
                    if not (isinstance(j, int) and j < 2):
                        pe.wait_ge(s.h_out, j - 1)
                    for a, (xs, ws) in enumerate(((XT_hi, W1_hi), (XT_hi, W1_lo), (XT_lo, W1_hi))):
                        mm = pe.matmul(bank[1 + p][:, :], xs[:, p, :], ws[:, bass.ds(e * DFF, DFF)],
                                       start=(a == 0), stop=(a == 2))
                    mm.then_inc(s.h_mm, 1)
                    if ahead:
                        load_expert(q, r + 1)
                if th:
                    pe.wait_ge(s.h_out, j)
                    if not (isinstance(j, int) and j < 3):
                        pe.wait_ge(s.ht_out, j - 2)
                    for c in range(FC):
                        mm = pe.transpose(bank[3 + (1 - p)][:, c * P:(c + 1) * P],
                                          Hs[:, 1 - p, c * P:(c + 1) * P], ident)
                    mm.then_inc(s.ht_mm, 1)
                if tx:
                    turn_x(j + 2, (r + 2) % RING, q + (r + 2) // RING)
                if w2:
                    e2 = expert(r - 2)
                    pe.wait_ge(s.ht_out, j - 1)
                    if not (isinstance(j, int) and j < 4):
                        pe.wait_ge(s.y_out, j - 3)
                    for c in range(FC):
                        mm = pe.matmul(bank[5 + p][:, 0:D], HT[:, p, c, :],
                                       W2[:, bass.ds(e2 * (FC * D) + c * D, D)],
                                       start=(c == 0), stop=(c == FC - 1))
                    mm.then_inc(s.y_mm, 1)

            pe.wait_ge(s.routed, PARTS)
            pe.wait_ge(w1_lo_set, 2 * (n + 1))
            if n == 0:
                pe.wait_ge(ffn_w_in, 16)
            turn_x(0, 0, 0)
            turn_x(1, 1, 0)
            load_expert(0, 0)
            for j in range(RING):
                slot(0, j, th=j >= 1, w2=j >= 2)
            with pe.Fori(1, NG // RING - 1) as q:
                for r in range(RING):
                    slot(q, r)
            for r in range(RING):
                slot(NG // RING - 1, r, tx=r < 2, ahead=r < RING - 1)
            slot(NG // RING, 0, w1=False, tx=False)
            slot(NG // RING, 1, w1=False, th=False, tx=False)

        def turn_rows(pe, s, g):
            pe.wait_ge(s.normed, ROW * (g + 1))
            if g >= 2:
                pe.wait_ge(s.turned_out, g - 1)
            for k in range(ROW):
                mm = pe.transpose(bank[g % 2][:, k * P:(k + 1) * P], XN[:, g * ROW + k, 0:D], ident)
            mm.then_inc(s.turned, 1)

        def rank(pe, s, part):
            pe.wait_ge(s.onehot, part + 1)
            cols = slice(part * PT * EXPERTS, (part + 1) * PT * EXPERTS)
            pe.matmul(bank[3][:, cols], lower, R[:, 3, cols], start=True, stop=True)
            pe.matmul(bank[4][:, cols], ones_sq, R[:, 3, cols], start=True, stop=True).then_inc(s.ranked, 1)

        def logits(pe, s, g):
            pe.wait_ge(s.turned_out, g + 1)
            for k in range(ROW):
                t = g * ROW + k
                mm = pe.matmul(bank[LOGIT_BANK][:, t * EXPERTS:(t + 1) * EXPERTS], XNT[:, g % 2, k * P:(k + 1) * P],
                               Wr[:, :], start=True, stop=True)
            mm.then_inc(s.logits, 1)

        def of_part(part):
            return slice(part * PT, (part + 1) * PT)

        def act_sqrt(act, sl, var_ready, count, sqrt_ready):
            act.wait_ge(var_ready, count)
            act.activation(ln[:, 1, sl], ln[:, 0, sl], ACT.Sqrt).then_inc(sqrt_ready, 1)

        def turned_out(act, s, g):
            act.wait_ge(s.turned, g + 1)
            if g >= 2:
                act.wait_ge(s.logits, g - 1)
            act.activation(XNT[:, g % 2, :], bank[g % 2][:, :], ACT.Copy).then_inc(s.turned_out, 1)

        def ffn_scalar(act, s, n):
            def exps(part):
                cols = slice(part * PT * EXPERTS, (part + 1) * PT * EXPERTS)
                act.wait_ge(s.shifted, part + 1)
                act.activation(R[:, 4, cols], R[:, 1, cols], ACT.Exp).then_inc(s.exped, 1)

            if n == 0:
                act_sqrt(act, of_part(0), s.var_ready, 1, s.sqrt_ready)
                for g in range(PT // ROW):
                    turned_out(act, s, g)
                act_sqrt(act, of_part(1), s.var_ready, 2, s.sqrt_ready)
                act.wait_ge(w1_in, 16 * 2)
                for k in range(2):
                    act.activation(W1_hi[:, k * W1_HALF:(k + 1) * W1_HALF], W1_raw[k], ACT.Copy
                                   ).then_inc(w1_hi_set, 1)
                exps(0)
            else:
                exps(0)
                act_sqrt(act, of_part(1), s.var_ready, 2, s.sqrt_ready)
            for g in range(PT // ROW, TILES // ROW):
                turned_out(act, s, g)
            exps(1)

            def copy_x(j, p):
                act.wait_ge(s.xt_mm, j + 1)
                if not (isinstance(j, int) and j < 2):
                    act.wait_ge(s.h_mm, j - 1)
                act.activation(XT_hi[:, p, :], bank[X_BANK[p]][:, 0:P], ACT.Copy).then_inc(s.xt_hi_out, 1)

            def slot(j, p, xt=True):
                act.wait_ge(s.h_mm, j + 1)
                if not (isinstance(j, int) and j < 2):
                    act.wait_ge(s.ht_mm, j - 1)
                act.activation(Hs[:, p, :], bank[1 + p][:, :], ACT.Copy).then_inc(s.h_out, 1)
                if xt:
                    copy_x(j + 2, p)

            copy_x(0, 0)
            copy_x(1, 1)
            slot(0, 0)
            slot(1, 1)
            with act.Fori(1, NG // 2 - 2) as q:
                for p in range(2):
                    slot(q * 2 + p, p)
            slot(NG - 4, 0)
            if n == 0:
                act_sqrt(act, slice(0, PT - RING), ln2_var, 1, ln2_sqrt)
            slot(NG - 3, 1)
            slot(NG - 2, 0, xt=False)
            slot(NG - 1, 1, xt=False)

        def norm_stats(dve, sl, s_var, s_sqrt, count):
            link(dve, dve.tensor_scalar(ln[:, 0, sl], mv[:, sl, 1], EPS, None, ALU.add))
            dve.drain().then_inc(s_var, 1)
            dve.wait_ge(s_sqrt, count)
            link(dve, dve.reciprocal(ln[:, 2, sl], ln[:, 1, sl]))
            link(dve, dve.tensor_tensor(ln[:, 3, sl], ln[:, 0, sl], ln[:, 2, sl], ALU.mult))
            link(dve, dve.tensor_tensor(ln[:, 4, sl], ln[:, 1, sl], ln[:, 3, sl], ALU.add))
            link(dve, dve.tensor_scalar(ln[:, 3, sl], ln[:, 4, sl], 0.5, None, ALU.mult))
            link(dve, dve.reciprocal(rstd[:, sl], ln[:, 3, sl]))

        def row_stats(dve, part):
            for t in range(part * PT, (part + 1) * PT):
                if t % 8 == 0:
                    dve.wait_ge(x_in[t // 8], 16)
                ins = dve.bn_stats(stats[:, t, :], X[:, t, :])
            link(dve, ins)

        def aggregate(dve, tiles):
            for t in tiles:
                ins = dve.bn_aggr(mv[:, t, :], stats[:, t, :])
            link(dve, ins)

        def normalise(dve, s, tiles):
            for t in tiles:
                dve.tensor_scalar(XN[:, t, 0:D], X[:, t, :], mv[:, t, 0:1], rstd[:, t:t + 1],
                                  ALU.subtract, ALU.mult).then_inc(s.normed, 1)

        def split_w1(dve, n):
            dve.wait_ge(w1_in, 16 * 2 * (n + 1))
            dve.wait_ge(w1_hi_set, 2)
            for k in range(2):
                cols = slice(k * W1_HALF, (k + 1) * W1_HALF)
                dve.tensor_tensor(W1_lo[:, cols], W1_raw[k], W1_hi[:, cols].bitcast(F32), ALU.subtract
                                  ).then_inc(w1_lo_set, 1)

        def ffn_vector(dve, s, n):
            if n == 0:
                for part in range(PARTS):
                    row_stats(dve, part)
                    aggregate(dve, range(part * PT, (part + 1) * PT))
                    norm_stats(dve, of_part(part), s.var_ready, s.sqrt_ready, part + 1)
                    normalise(dve, s, range(part * PT, (part + 1) * PT))
                route(dve, s, n, 0)
                split_w1(dve, n)
                route(dve, s, n, 1)
            else:
                dve.wait_ge(wo_added, BATCH)
                for t in range(TILES - QT, TILES):
                    ins = dve.bn_stats(stats[:, t, :], X[:, t, :])
                link(dve, ins)
                aggregate(dve, range(TILES - QT, TILES))
                norm_stats(dve, of_part(1), s.var_ready, s.sqrt_ready, 2)
                normalise(dve, s, range(PT, TILES))
                split_w1(dve, n)
                route(dve, s, n, 1)
            multiply(dve, s, n)

        def route(dve, s, n, part):
            if n == 0 and part == 0:
                dve.wait_ge(b1_turned, 1)
                dve.tensor_copy(b1_col[:, :], bank[5][:, 0:EXPERTS * FC]).then_inc(b1_set, 1)
                dve.wait_ge(b1_set, 1)
                dve.wait_ge(con_in, 16)
                dve.wait_ge(small_in, 16 * 4)

            def te(ap):
                return ap.rearrange("p (t e) -> p t e", e=EXPERTS)

            def et(ap):
                return ap.rearrange("p (e t) -> p e t", t=PT)

            def by_tile(v):
                return v.unsqueeze(2).to_broadcast([P, PT, EXPERTS])

            full = [P, PT, EXPERTS]
            desc = con[:, C_DESC:C_DESC + EXPERTS].unsqueeze(1).to_broadcast(full)
            sl = of_part(part)
            cols = slice(part * PT * EXPERTS, (part + 1) * PT * EXPERTS)
            lg, sh, cand, oh, ex, cnt, inc, exc = (R[:, k, cols] for k in range(8))
            mx, cm, se = (small[:, k, sl] for k in range(3))
            n_of, n_tiles, upto, before, adj = (small[:, k, part * PT:part * PT + EXPERTS] for k in range(3, 8))
            place_f, gate = small[:, 8, sl], small[:, 9, sl]
            dve.wait_ge(s.logits, (part + 1) * PT // ROW)
            link(dve, dve.tensor_tensor(te(lg), te(bank[LOGIT_BANK][:, cols]),
                                        br_all[:, :].unsqueeze(1).to_broadcast(full), ALU.add))
            link(dve, dve.tensor_reduce(mx, te(lg), AX.X, ALU.max))
            dve.tensor_tensor(te(sh), te(lg), by_tile(mx), ALU.subtract).then_inc(s.shifted, 1)
            link(dve, dve.tensor_tensor(te(cand), te(lg), by_tile(mx), ALU.is_equal))
            link(dve, dve.tensor_tensor(te(cand), te(cand), desc, ALU.mult))
            link(dve, dve.tensor_reduce(cm, te(cand), AX.X, ALU.max))
            dve.tensor_tensor(te(oh), te(cand), by_tile(cm), ALU.is_equal).then_inc(s.onehot, 1)
            dve.wait_ge(s.ranked, part + 1)
            link(dve, dve.tensor_copy(et(cnt), te(bank[4][:, cols]).rearrange("p t e -> p e t")))
            dve.wait_ge(const_set, 3)
            link(dve, dve.tensor_tensor_scan(inc, ones[:, :], cnt, 0.0, ALU.mult, ALU.add))
            link(dve, dve.tensor_tensor(exc, inc, cnt, ALU.subtract))
            link(dve, dve.tensor_reduce(n_of, et(cnt), AX.X, ALU.add))
            thr = con[:, C_THR:C_THR + PT].unsqueeze(1).to_broadcast([P, EXPERTS, PT])
            link(dve, dve.tensor_tensor(et(cand), n_of.unsqueeze(2).to_broadcast([P, EXPERTS, PT]), thr, ALU.is_gt))
            link(dve, dve.tensor_reduce(n_tiles, et(cand), AX.X, ALU.add))
            link(dve, dve.tensor_tensor_scan(upto, ones[:, 0:EXPERTS], n_tiles, 0.0, ALU.mult, ALU.add))
            link(dve, dve.tensor_tensor(before, upto, n_tiles, ALU.subtract))
            link(dve, dve.scalar_tensor_tensor(out=adj, in0=before, scalar=float(P), in1=et(exc)[:, :, 0],
                                               op0=ALU.mult, op1=ALU.subtract))
            link(dve, dve.tensor_tensor(et(inc), et(exc), adj.unsqueeze(2).to_broadcast([P, EXPERTS, PT]), ALU.add))
            link(dve, dve.tensor_tensor(te(cand), te(bank[3][:, cols]),
                                        et(inc).rearrange("p e t -> p t e"), ALU.add))
            link(dve, dve.tensor_tensor(cand, cand, oh, ALU.mult))
            link(dve, dve.tensor_reduce(place_f, te(cand), AX.X, ALU.add))
            dve.tensor_copy(place[:, sl], place_f).then_inc(s.placed, 1)
            tiles = slice(part * NGP, (part + 1) * NGP)
            le = [P, NGP, EXPERTS - 1]
            link(dve, dve.tensor_tensor(first_le[:, part, :, :], upto[:, 0:EXPERTS - 1].unsqueeze(1).to_broadcast(le),
                                        con[:, C_TIX:C_TIX + NGP].unsqueeze(2).to_broadcast(le), ALU.is_le))
            link(dve, dve.tensor_reduce(expert_f[:, tiles], first_le[:, part, :, :], AX.X, ALU.add))
            dve.tensor_copy(expert_of[:, tiles], expert_f[:, tiles]).then_inc(s.routed, 1)
            dve.wait_ge(s.exped, part + 1)
            link(dve, dve.tensor_reduce(se, te(ex), AX.X, ALU.add))
            link(dve, dve.reciprocal(gate, se))
            link(dve, dve.tensor_scalar(half_gate[:, sl], gate, 0.5, None, ALU.mult))

        def add_back(dve, s, t):
            row = slice(t, t + 1) if isinstance(t, int) else bass.ds(t, 1)
            dve.scalar_tensor_tensor(out=X[:, row, :].squeeze(1), in0=XN[:, row, 0:D].squeeze(1),
                                     scalar=half_gate[:, row], in1=X[:, row, :].squeeze(1),
                                     op0=ALU.mult, op1=ALU.add).then_inc(s.added, 1)

        def multiply(dve, s, n):
            dve.wait_ge(s.routed, PARTS)
            experts = [dve.alloc_register(f"dve_f{n}_expert{r}") for r in range(RING)]

            def load_expert(q, r):
                dve.reg_load(experts[r % RING], expert_of[0:1, bass.ds(q * RING + r, 1)])

            def expert(r):
                return dve.snap(experts[r % RING], min_val=0, max_val=EXPERTS - 1)

            def relu(q, r, ahead=True):
                j, p = q * RING + r, r % 2
                e = expert(r)
                dve.wait_ge(s.ht_mm, j + 1)
                if not (isinstance(j, int) and j < 2):
                    dve.wait_ge(s.y_mm, j - 1)
                for c in range(FC):
                    ins = dve.tensor_scalar(HT[:, p, c, :], bank[3 + p][:, c * P:(c + 1) * P],
                                            b1_col[:, bass.ds(e * FC + c, 1)], 0.0, ALU.add, ALU.max)
                ins.then_inc(s.ht_out, 1)
                if ahead:
                    load_expert(q, r + 1)

            def x_lo(j, r, tokens=False):
                dve.wait_ge(s.xt_hi_out, j + 1)
                if tokens:
                    dve.tensor_copy(token[:, bass.ds(j - (NGP - 1), 1)], XG[:, r % RING, D:D + 1]
                                    ).then_inc(s.token_set, 1)
                if not (isinstance(j, int) and j < 2):
                    dve.wait_ge(s.h_mm, j - 1)
                dve.tensor_tensor(XT_lo[:, r % 2, :], bank[X_BANK[r % 2]][:, 0:P], XT_hi[:, r % 2, :].bitcast(F32),
                                  ALU.subtract).then_inc(s.xt_lo_out, 1)

            def add_b2(j, r, stores, sent=False):
                e = expert(r)
                dve.wait_ge(s.y_mm, j + 1)
                if sent:
                    dve.wait_ge(s.y_sent[r], (stores - NGP // RING) * 16)
                elif stores is not None:
                    dve.wait_ge(s.y_stored[r], stores * 16)
                dve.tensor_tensor(Y[:, r, :], bank[5 + r % 2][:, 0:D], b2_all[:, bass.ds(e * D, D)],
                                  ALU.add).then_inc(s.y_out, 1)

            load_expert(0, 0)
            for j in range(3):
                x_lo(j, j)
            for j in range(RING):
                relu(0, j)
                x_lo(j + 3, j + 3)
                if j >= 1:
                    add_b2(j - 1, j - 1, None)
            last = NG // RING - 1
            back = NG // RING - PT // RING

            def turn(q, groups, end=False, tokens=False, sent=False):
                for r in range(RING):
                    relu(q, r, ahead=not (end and r == RING - 1))
                    if not end or r + 3 < RING:
                        x_lo(q * RING + (r + 3), r + 3, tokens)
                    t = (q - back) * RING + r
                    if groups:
                        add_back(dve, s, t)
                    add_b2(q * RING + (r - 1), (r - 1) % RING, q if r else q - 1,
                           sent=sent or (n == 1 and isinstance(q, int) and q == NGP // RING + 1 and r >= 1))
                    if groups:
                        if n == 0:
                            dve.wait_ge(s.added, t + 1)
                            dve.bn_stats(stats[:, bass.ds(t, 1), :].squeeze(1),
                                         X[:, bass.ds(t, 1), :].squeeze(1)).then_inc(s.measured, 1)

            half_back = back + PT // RING // 2
            ranges = ((back, half_back, (0, 1)), (half_back, last, (2, 3)))
            part_1 = NGP // RING
            if n == 0:
                ranges = ((1, back, ()),) + ranges
            else:
                ranges = ((1, part_1 - 1, ()), (part_1 - 1, part_1 + 1, ())) + ranges
            for first, end, groups in ranges:
                if n == 1 and first == back:
                    for q in range(part_1 + 1, back):
                        turn(q, (), tokens=True)
                for g in groups:
                    dve.wait_ge(s.gathered[g], 16 * ROW)
                with dve.Fori(first, end) as q:
                    turn(q, groups, tokens=n == 1 and first >= part_1 - 1, sent=n == 1 and first >= back)
            if n == 0:
                dve.wait_ge(s.measured, PT - RING)
                aggregate(dve, range(PT - RING))
                norm_stats(dve, slice(0, PT - RING), ln2_var, ln2_sqrt, 1)
            turn(last, (2, 3), end=True, tokens=n == 1, sent=n == 1)
            add_b2(NG - 1, RING - 1, NG // RING - 1, sent=n == 1)

        def ffn_gpsimd(pool, s, n):
            for part in range(PARTS):
                pool.wait_ge(s.placed, part + 1)
                pool.wait_ge(zero_fill, 16 * (PARTS if n == 0 else PARTS + 1))
                for t in range(part * PT, (part + 1) * PT):
                    pool.indirect_dma_start(out=grouped_x[part], out_offset=bass.IndirectOffsetOnAxis(ap=place[:, t:t + 1], axis=0),
                                            in_=XN[:, t, 0:WIDTH[part]], in_offset=None).then_inc(s.scattered[part], 16)
            if n == 0:
                pool.wait_ge(attn_w_in, 16 * 7)
                pool.tensor_copy(w_hi[:, :, :], w_raw[:, :, :]).then_inc(w_hi_set, 1)
                pool.wait_ge(w_hi_set, 1)
                pool.tensor_tensor(w_lo[:, :, :], w_raw[:, :, :], w_hi[:, :, :].bitcast(F32),
                                   ALU.subtract).then_inc(w_lo_set, 1)
            results_stored(pool, s, 0)
            for t in range(PT if n == 0 else AHEAD):
                gather(pool, s, t)
            if n == 1:
                for k in range(NGP):
                    pool.wait_ge(s.y_out, NGP + k + 1)
                    pool.wait_ge(s.token_set, k + 2)
                    pool.indirect_dma_start(out=results, out_offset=bass.IndirectOffsetOnAxis(ap=token[:, k + 1:k + 2], axis=0),
                                            in_=Y[:, k % RING, :], in_offset=None).then_inc(s.y_sent[k % RING], 16)
                    if AHEAD + k < PT:
                        gather(pool, s, AHEAD + k)

        def results_stored(pool, s, part):
            for r in range(RING):
                pool.wait_ge(s.y_stored[r], 16 * (part + 1) * (NGP // RING))
            pool.wait_ge(s.scattered[part], 16 * PT)

        def gather(pool, s, t):
            pool.indirect_dma_start(out=XN[:, t, 0:D], out_offset=None, in_=grouped_y[t // PT],
                                    in_offset=bass.IndirectOffsetOnAxis(ap=place[:, t:t + 1], axis=0)
                                    ).then_inc(s.gathered[t // ROW], 16)

        WO_BANK, LAST_WO_BANK, TX_BANK, QK_BANK = 6, 7, 0, 6
        FIRST_QK_BANK = (4, 5, 6)
        ACT_PROBS = (0, 6, 8, 10)
        REST_AT = 1 + PT // 4
        V_AT = ((4, 5), (4, 7))
        PROB_LAG, TURN_LAG, PV_LAG = 2, 3, 4

        def behind(b, h, lag):
            return (b - 1, h - lag + HEADS) if h < lag else (b, h - lag)

        def pe_turn_x(pe, b, first=False):
            pe.wait_ge(xn_set, b + 1)
            if not first:
                pe.wait_ge(v_set, 4 * b - 1)
            for t in range(QT):
                mm = pe.transpose(bank[TX_BANK][:, t * P:(t + 1) * P], xn[:, t, :], ident)
            mm.then_inc(xT_mm, 1)

        def pe_project(pe, tau, half, m):
            kind, t = m // QT, m % QT
            bk = m % 2
            n = tau if isinstance(tau, int) else tau[0]
            if m == 0:
                pe.wait_ge(xT_lo_set, (tau - half) // 2 + 1 if isinstance(tau, int) else tau[1] + 1)
                if half == 1:
                    pe.wait_ge(v_set, 2 * n - 1)
            elif m == 1:
                if not (isinstance(n, int) and n == 0):
                    pe.wait_ge(v_set, 2 * n)
            else:
                pe.wait_ge(rope_w, 4 * n + m - 1)
            for a, (xs, ws) in enumerate(((xT_hi, w_hi), (xT_hi, w_lo), (xT_lo, w_hi))):
                mm = pe.matmul(bank[bk][:, :], xs[:, t * P:(t + 1) * P], ws[:, 2 * kind + half, :],
                               start=(a == 0), stop=(a == 2))
            mm.then_inc(proj_mm, 1)

        def pe_turn_qk(pe, n, half, j, wo_before=None, at=QK_BANK):
            if j == 0:
                pe.wait_ge(rot_set, 4 * n + 4)
            if not (isinstance(n, int) and n == 0 and j < 3):
                pe.wait_ge(qk_lo_set, 4 * n + j)
            if wo_before is not None:
                pe.wait_ge(wo_added, wo_before)
            for kind in range(2):
                for t in range(QT):
                    mm = pe.transpose(bank[at][:, (kind * QT + t) * P:(kind * QT + t + 1) * P],
                                      rot[:, kind, t, j * P:(j + 1) * P], ident)
            mm.then_inc(turn_mm, 1)

        def pe_scores(pe, b, h, first=False):
            half, i = h // HALF, h % HALF
            j, at = i // 2, HEAD * (i % 2)
            if i % 2 == 0:
                pe.wait_ge(qk_lo_set, 8 * b + 4 * half + j + 1)
            if not first:
                pe.wait_ge(exp_set, HEADS * b + h - 1)
            q = [a[at:at + HEAD, half, j, 0, :] for a in (qk_hi, qk_lo)]
            k = [a[at:at + HEAD, half, j, 1, :] for a in (qk_hi, qk_lo)]
            for t in range(QT):
                for a, (x1, x2) in enumerate(((0, 0), (0, 1), (1, 0))):
                    mm = pe.matmul(bank[2 + h % 2][:, t * SEQ:(t + 1) * SEQ], q[x1][:, t * P:(t + 1) * P], k[x2],
                                   start=(a == 0), stop=(a == 2))
            mm.then_inc(score_mm, 1)

        def pe_turn_e(pe, b, h, first=False):
            if h in ACT_PROBS:
                pe.wait_ge(prob_act_set, len(ACT_PROBS) * b + ACT_PROBS.index(h) + 1)
            else:
                own = HEADS - len(ACT_PROBS)
                pe.wait_ge(prob_set, own * b + h + 1 - sum(k < h for k in ACT_PROBS))
            if not first:
                pe.wait_ge(et_set, HEADS * b + h - 1)
            for kt in range(QT):
                for t in range(QT):
                    mm = pe.transpose(bank[4 + h % 2][:, kt * SEQ + t * P:kt * SEQ + (t + 1) * P],
                                      E[:, h % 4, t, kt * P:(kt + 1) * P], ident)
            mm.then_inc(et_mm, 1)

        def pe_pv(pe, b, h, first=False):
            half, i = h % HEADS // HALF, h % HALF
            at = HEAD * (i % 2)
            pe.wait_ge(et_set, HEADS * b + h + 1)
            if i == 0:
                pe.wait_ge(v_set, 4 * b + 2 * half + 2)
            if i % 2 == 0 and not first:
                pe.wait_ge(ot_set, 8 * b + h // 2)
            for kt in range(QT):
                mm = pe.matmul(bank[7][at:at + HEAD, 0:SEQ], V[:, half, kt, i * HEAD:(i + 1) * HEAD],
                               ET[:, h % 2, kt * SEQ:(kt + 1) * SEQ], start=(kt == 0), stop=(kt == QT - 1))
            mm.then_inc(pv_mm, 1)

        def pe_wo(pe, b, b_prev, last=False):
            pe.wait_ge(ot_set, 8 * (b_prev + 1))
            if not last:
                pe.wait_ge(qk_lo_set, 8 * b + 4)
            for t in range(QT):
                for j in range(HEADS // 2):
                    mm = pe.matmul(bank[LAST_WO_BANK if last else WO_BANK][:, t * D:(t + 1) * D], OT[:, j, t * P:(t + 1) * P], Wo[:, j, :],
                                   start=(j == 0), stop=(j == HEADS // 2 - 1))
            mm.then_inc(wo_mm, 1)

        def pe_batch(pe, b, first=False, last=False):
            for half in range(2):
                prep = not (last and half == 1)
                tau = 2 * b + half + 1
                tgt = 1 - half
                tb = (tau, b + half)
                for i in range(HALF):
                    h = HALF * half + i
                    pe_scores(pe, b, h, first=first and h < 2)
                    if not (first and h < TURN_LAG):
                        pe_turn_e(pe, *behind(b, h, TURN_LAG), first=first and h - TURN_LAG < 2)
                    if i == 1:
                        pe_turn_qk(pe, 2 * b + half, half, 3)
                    if prep and (i < 4 or i in V_AT[half]):
                        pe_project(pe, tb, tgt, i if i < 4 else 4 + V_AT[half].index(i))
                    if not (first and h < PV_LAG):
                        pe_pv(pe, *behind(b, h, PV_LAG), first=first and h - PV_LAG < 2)
                    if half == 0 and i == 4 and not first:
                        pe_wo(pe, b, b - 1)
                    if half == 0 and i == 6 and not last:
                        pe_turn_x(pe, b + 1)
                    if last and half == 1 and i >= HALF - PT // ROW:
                        g = i - (HALF - PT // ROW)
                        if g == 0:
                            pe.wait_ge(v_set, 2 * 2 * BATCH)
                            pe.wait_ge(qk_lo_set, 4 * 2 * BATCH)
                        turn_rows(pe, ffn[1], g)
                        if g >= 1:
                            logits(pe, ffn[1], g - 1)
                    if prep and i >= 5:
                        pe_turn_qk(pe, tau, tgt, i - 5, wo_before=b if i == 5 and half == 0 and not first else None)

        def attention_tensor(pe):
            pe.wait_ge(w_lo_set, 1)
            pe_turn_x(pe, 0, first=True)
            for m in range(6):
                pe_project(pe, 0, 0, m)
            for j in range(PAIRS - 1):
                pe_turn_qk(pe, 0, 0, j, at=FIRST_QK_BANK[j])
            pe_batch(pe, 0, first=True)
            with pe.Fori(1, BATCH - 1) as b:
                pe_batch(pe, b)
            pe_batch(pe, BATCH - 1, last=True)
            for h in range(HEADS, HEADS + PV_LAG):
                if h - TURN_LAG < HEADS:
                    pe_turn_e(pe, BATCH - 1, h - TURN_LAG)
                pe_pv(pe, BATCH - 1, h - PV_LAG)
                if h == HEADS:
                    logits(pe, ffn[1], PT // ROW - 1)
            rank(pe, ffn[1], 0)
            pe_wo(pe, BATCH, BATCH - 1, last=True)

        def act_hi(act, n, half, j, at=QK_BANK):
            act.wait_ge(turn_mm, 4 * n + j + 1)
            act.activation(qk_hi[:, half, j, :, :], bank[at][:, :].rearrange("p (k s) -> p k s", k=2),
                           ACT.Copy).then_inc(qk_hi_set, 1)

        def act_v(act, n, half, t):
            act.wait_ge(proj_mm, 6 * n + 5 + t)
            act.activation(V[:, half, t, :], bank[t % 2][:, :], ACT.Copy).then_inc(v_set, 1)

        def act_x_hi(act, b):
            act.wait_ge(xT_mm, b + 1)
            act.activation(xT_hi[:, :], bank[TX_BANK][:, 0:SEQ], ACT.Copy).then_inc(xT_hi_set, 1)

        def act_ot(act, b, j, first=False):
            act.wait_ge(pv_mm, HEADS * b + 2 * j + 2)
            if not first:
                act.wait_ge(wo_mm, b)
            act.activation(OT[:, j, :], bank[7][:, 0:SEQ], ACT.Copy).then_inc(ot_set, 1)

        def act_et(act, b, h, first=False):
            act.wait_ge(et_mm, HEADS * b + h + 1)
            if not first:
                act.wait_ge(pv_mm, HEADS * b + h - 1)
            act.activation(ET[:, h % 2, :], bank[4 + h % 2][:, :], ACT.Copy).then_inc(et_set, 1)

        def act_exp(act, b, h, first=False):
            act.wait_ge(max_set, HEADS * b + h + 1)
            if not first:
                act.wait_ge(et_mm, HEADS * b + h - 3)
            for t in range(QT):
                ins = act.activation(E[:, h % 4, t, :], bank[2 + h % 2][:, t * SEQ:(t + 1) * SEQ], ACT.Exp,
                                     bias=negmax[:, h % 2, t:t + 1], accum_out=total[:, h % 2, t:t + 1])
            ins.then_inc(exp_set, 1)

        def act_prob(act, b, h):
            act.wait_ge(recip_set, HEADS * b + h + 1)
            for t in range(QT):
                ins = act.activation(E[:, h % 4, t, :], E[:, h % 4, t, :], ACT.Copy, scale=recip[:, h % 2, t:t + 1])
            ins.then_inc(prob_act_set, 1)

        def act_batch(act, b, first=False, last=False):
            for half in range(2):
                prep = not (last and half == 1)
                tau = 2 * b + half + 1
                tgt = 1 - half
                for i in range(HALF):
                    h = HALF * half + i
                    if last and half == 1 and i > HALF - PT // ROW:
                        turned_out(act, ffn[1], i - (HALF - PT // ROW) - 1)
                    if i == 0 or i == 3:
                        act_hi(act, 2 * b + half, half, 2 if i == 0 else 3)
                    if prep and i >= 6:
                        act_hi(act, tau, tgt, i - 6)
                    if h % 2 == 0 and not (first and h < PV_LAG + 2):
                        eb, eh = behind(b, h, PV_LAG + 2)
                        act_ot(act, eb, eh // 2, first=first)
                    if not (first and h < 1):
                        act_exp(act, *behind(b, h, 1), first=first and h < 5)
                    if not (first and h < TURN_LAG):
                        act_et(act, *behind(b, h, TURN_LAG), first=first and h - TURN_LAG < 2)
                    if (h - PROB_LAG) % HEADS in ACT_PROBS and not (first and h < PROB_LAG):
                        act_prob(act, *behind(b, h, PROB_LAG))
                    if prep and i in V_AT[half]:
                        act_v(act, tau, tgt, V_AT[half].index(i))
                    if half == 0 and i == 6 and not last:
                        act_x_hi(act, b + 1)
                    if last and half == 1 and i == 1:
                        act_sqrt(act, of_part(0), ffn[1].var_ready, 1, ffn[1].sqrt_ready)

        def attention_scalar(act):
            act_x_hi(act, 0)
            for t in range(QT):
                act_v(act, 0, 0, t)
            for j in range(PAIRS - 2):
                act_hi(act, 0, 0, j, at=FIRST_QK_BANK[j])
            act_batch(act, 0, first=True)
            with act.Fori(1, REST_AT) as b:
                act_batch(act, b)
            act_sqrt(act, slice(PT - RING, TILES), ln2_var, 2, ln2_sqrt)
            act.activation(ln[:, 4, 0:1], ones[:, 0:1], ACT.Exp)
            with act.Fori(REST_AT, BATCH - 1) as b:
                act_batch(act, b)
            act_batch(act, BATCH - 1, last=True)
            for h in range(HEADS, HEADS + PV_LAG + 1):
                if h == HEADS:
                    turned_out(act, ffn[1], PT // ROW - 1)
                    act_exp(act, BATCH - 1, HEADS - 1)
                if h % 2 == 0:
                    act_ot(act, BATCH - 1, (h - PV_LAG - 2) // 2)
                if h - TURN_LAG < HEADS:
                    act_et(act, BATCH - 1, h - TURN_LAG)

        def dve_xn(dve, b, first=False):
            if not first:
                dve.wait_ge(xT_mm, b)
            for t in range(QT):
                tile = b * QT + t
                ins = dve.tensor_scalar(xn[:, t, :], X[:, bass.ds(tile, 1), :].squeeze(1) if not isinstance(b, int) else X[:, tile, :],
                                        mv[:, bass.ds(tile, 1), 0:1].squeeze(1), rstd[:, bass.ds(tile, 1)],
                                        ALU.subtract, ALU.mult)
            ins.then_inc(xn_set, 1)

        def dve_x_lo(dve, b):
            dve.wait_ge(xT_hi_set, b + 1)
            dve.tensor_tensor(xT_lo[:, :], bank[TX_BANK][:, 0:SEQ], xT_hi[:, :].bitcast(F32),
                              ALU.subtract).then_inc(xT_lo_set, 1)

        def dve_rope(dve, n, half, m, first=False):
            kind, t = m // QT, m % QT
            dve.wait_ge(proj_mm, 6 * n + m + 1)
            if not (first and m < 2):
                dve.wait_ge(rot_set, 4 * n + m - 1)
            src = bank[m % 2][:, :]
            pb = m % 2
            dve.tensor_tensor(rot_u[:, pb, :].rearrange("p (h d) -> p h d", d=HEAD),
                              src.rearrange("p (h d) -> p h d", d=HEAD),
                              table(kind, 0, t).unsqueeze(1).to_broadcast([P, HALF, HEAD]), ALU.mult)
            dve.tensor_tensor(rot_w[:, pb, :].rearrange("p (h j d) -> p h j d", j=2, h=HALF)[:, :, ::-1, :],
                              src.rearrange("p (h j d) -> p h j d", j=2, h=HALF),
                              table(kind, 1, t).rearrange("p (j d) -> p j d", j=2).unsqueeze(1)
                              .to_broadcast([P, HALF, 2, HEAD // 2]), ALU.mult).then_inc(rope_w, 1)

        def dve_lo(dve, n, half, j, at=QK_BANK):
            dve.wait_ge(qk_hi_set, 4 * n + j + 1)
            dve.tensor_tensor(qk_lo[:, half, j, :, :], bank[at][:, :].rearrange("p (k s) -> p k s", k=2),
                              qk_hi[:, half, j, :, :].bitcast(F32), ALU.subtract).then_inc(qk_lo_set, 1)

        def dve_max(dve, b, h):
            dve.wait_ge(score_mm, HEADS * b + h + 1)
            dve.tensor_reduce(negmax[:, h % 2, :], bank[2 + h % 2][:, :].rearrange("p (t s) -> p t s", t=QT),
                              AX.X, ALU.max, negate=True).then_inc(max_set, 1)

        def dve_prob(dve, b, h):
            dve.wait_ge(exp_set, HEADS * b + h + 1)
            dve.reciprocal(recip[:, h % 2, :], total[:, h % 2, :]).then_inc(recip_set, 1)
            if h in ACT_PROBS:
                return
            dve.wait_ge(recip_set, HEADS * b + h + 1)
            for t in range(QT):
                ins = dve.tensor_scalar(E[:, h % 4, t, :], E[:, h % 4, t, :], recip[:, h % 2, t:t + 1], None, ALU.mult)
            ins.then_inc(prob_set, 1)

        def dve_wo(dve, b, last=False):
            dve.wait_ge(wo_mm, b + 1)
            xs = X[:, bass.ds(b * QT, QT), :]
            dve.tensor_tensor(xs, bank[LAST_WO_BANK if last else WO_BANK][:, 0:QT * D].rearrange("p (t d) -> p t d", t=QT), xs,
                              ALU.add).then_inc(wo_added, 1)

        def dve_measure(dve, b):
            dve.wait_ge(wo_added, b + 1)
            for t in range(QT):
                row = bass.ds(b * QT + t, 1)
                dve.bn_stats(stats[:, row, :].squeeze(1), X[:, row, :].squeeze(1)).then_inc(ffn[1].measured, 1)

        def dve_batch(dve, b, first=False, last=False, rest=False):
            for half in range(2):
                prep = not (last and half == 1)
                tau = 2 * b + half + 1
                tgt = 1 - half
                for i in range(HALF):
                    h = HALF * half + i
                    if i == 0 or (i == 4 and half == 0):
                        dve_lo(dve, 2 * b + half, half, 2 if i == 0 else 3)
                    if prep and i >= 6:
                        dve_lo(dve, tau, tgt, i - 6)
                    if not (first and h < PROB_LAG):
                        dve_prob(dve, *behind(b, h, PROB_LAG))
                    if i == 4 and half == 1:
                        dve_lo(dve, 2 * b + half, half, 3)
                    dve_max(dve, b, h)
                    if half == 0 and i == 5 and not first:
                        dve_wo(dve, b - 1)
                    if half == 0 and i == 4 and not last:
                        dve_xn(dve, b + 1)
                    if prep and i < 4:
                        dve_rope(dve, tau, tgt, i)
                    if half == 0 and i == 6 and not last:
                        dve_x_lo(dve, b + 1)
                    if half == 0 and i == 7 and not first:
                        dve_measure(dve, b - 1)
                    if last and half == 1 and i == 1:
                        dve.wait_ge(ffn[1].measured, PT)
                        aggregate(dve, range(PT))
                        norm_stats(dve, of_part(0), ffn[1].var_ready, ffn[1].sqrt_ready, 1)
                    if last and half == 1 and 2 <= i < 2 + PT // ROW:
                        normalise(dve, ffn[1], range((i - 2) * ROW, (i - 1) * ROW))
                    if half == 1 and i >= 4 and rest:
                        t = PT + (b - 1) * 4 + (i - 4)
                        add_back(dve, ffn[0], t)
                        dve.wait_ge(ffn[0].added, t + 1)
                        dve.bn_stats(stats[:, bass.ds(t, 1), :].squeeze(1),
                                     X[:, bass.ds(t, 1), :].squeeze(1)).then_inc(ffn[0].measured, 1)

        def attention_vector(dve):
            dve_xn(dve, 0, first=True)
            dve_x_lo(dve, 0)
            for m in range(4):
                dve_rope(dve, 0, 0, m, first=True)
            for j in range(PAIRS - 2):
                dve_lo(dve, 0, 0, j, at=FIRST_QK_BANK[j])
            dve_batch(dve, 0, first=True)
            for g in range(PT // ROW, TILES // ROW):
                dve.wait_ge(ffn[0].gathered[g], 16 * ROW)
            with dve.Fori(1, REST_AT) as b:
                dve_batch(dve, b, rest=True)
            dve.wait_ge(ffn[0].measured, TILES)
            aggregate(dve, range(PT - RING, TILES))
            norm_stats(dve, slice(PT - RING, TILES), ln2_var, ln2_sqrt, 2)
            with dve.Fori(REST_AT, BATCH - 1) as b:
                dve_batch(dve, b)
            dve_batch(dve, BATCH - 1, last=True)
            for h in range(HEADS - PROB_LAG, HEADS):
                dve_prob(dve, BATCH - 1, h)
            dve.wait_ge(ffn[1].measured, TILES - QT)
            route(dve, ffn[1], 1, 0)
            aggregate(dve, range(PT, TILES - QT))
            dve_wo(dve, BATCH - 1, last=True)
            dve.wait_ge(wo_added, BATCH)

        def pool_rot(pool, n, m):
            pool.wait_ge(rope_w, 4 * n + m + 1)
            if m == 0 and not (isinstance(n, int) and n == 0):
                pool.wait_ge(turn_mm, 4 * n)
            pool.tensor_tensor(rot[:, m // QT, m % QT, :], rot_u[:, m % 2, :], rot_w[:, m % 2, :],
                               ALU.add).then_inc(rot_set, 1)

        def attention_gpsimd(pool):
            pool.wait_ge(w_lo_set, 1)
            for m in range(4):
                pool_rot(pool, 0, m)
            results_stored(pool, ffn[0], 1)
            for n in range(1, 3):
                for m in range(4):
                    pool_rot(pool, n, m)
                for t in range(PT + (n - 1) * PT // 2, PT + n * PT // 2):
                    gather(pool, ffn[0], t)
            with pool.Fori(3, 2 * BATCH) as n:
                for m in range(4):
                    pool_rot(pool, n, m)

        def blank_rows(sp, k):
            sp.dma_start(grouped_x[k].rearrange("(n p) d -> p n d", p=P),
                         blank[:, 0:WIDTH[k]].unsqueeze(1).to_broadcast([P, NGP, WIDTH[k]])).then_inc(zero_fill, 16)

        def load_w1(sp):
            for k in range(2):
                sp.dma_start(W1_raw[k].rearrange("p (e f) -> p e f", e=EXPERTS // 2),
                             w1[k * EXPERTS // 2:(k + 1) * EXPERTS // 2].rearrange("e p f -> p e f")).then_inc(w1_in, 16)

        @block.sync
        def _(sp):
            sp.dma_start(con[:, :], consts).then_inc(con_in, 16)
            for g in range(4):
                sp.dma_start(X[:, 8 * g:8 * g + 8, :], x_t[:, 8 * g:8 * g + 8, :]).then_inc(x_in[g], 16)
            sp.dma_start(Wr[:, :], wr).then_inc(small_in, 16)
            sp.dma_start(br_all[:, :], br.rearrange("(a e) -> a e", a=1).to_broadcast([P, EXPERTS])).then_inc(small_in, 16)
            sp.dma_start(b1_rows[:, :], b1.rearrange("e (c p) -> (e c) p", p=P)).then_inc(small_in, 16)
            sp.dma_start(b2_all[:, :], b2.rearrange("(a e) d -> a (e d)", a=1).to_broadcast([P, EXPERTS * D])
                         ).then_inc(small_in, 16)
            sp.wait_ge(const_set, 1)
            for k in range(PARTS):
                blank_rows(sp, k)
            load_w1(sp)
            sp.dma_start(W2[:, :].rearrange("p (e c d) -> p e c d", e=EXPERTS, c=FC),
                         w2.rearrange("e (c p) d -> p e c d", p=P)).then_inc(ffn_w_in, 16)
            for k, w in enumerate((wq, wk, wv)):
                for half in range(2):
                    sp.dma_start(w_raw[:, 2 * k + half, :], w[:, 512 * half:512 * half + 512]).then_inc(attn_w_in, 16)
            sp.dma_start(Wo[:, :, :], wo.rearrange("(j p) d -> p j d", p=P)).then_inc(attn_w_in, 16)
            ffn_load_store(sp, ffn[0], 0)
            sp.dma_start(grouped_x[1].rearrange("(n p) d -> p n d", p=P)[:, :, D],
                         con[:, C_TOKEN + PT:C_TOKEN + PT + NGP], allow_slow_non_contiguous=True).then_inc(zero_fill, 16)
            sp.wait_ge(pv_mm, HEADS * BATCH)
            load_w1(sp)
            ffn_load_store(sp, ffn[1], 1)
            for r in range(RING):
                sp.wait_ge(ffn[1].y_sent[r], 16 * (NGP // RING))
            for g in range(PT // ROW, TILES // ROW):
                sp.dma_start(XN[:, ROW * g:ROW * g + ROW, 0:D],
                             results[P * (ROW * g - PT):P * (ROW * g - PT + ROW), :].rearrange("(n p) d -> p n d", p=P)
                             ).then_inc(ffn[1].gathered[g], 16)
            for g in range(TILES // ROW):
                sp.wait_ge(ffn[1].added, ROW * (g + 1))
                sp.dma_start(out_t[:, ROW * g:ROW * g + ROW, :], X[:, ROW * g:ROW * g + ROW, :]).then_inc(out_done, 16)
            sp.wait_ge(out_done, 16 * (TILES // ROW))

        @block.tensor
        def _(pe):
            pe.wait_ge(con_in, 16)
            ffn_tensor(pe, ffn[0], 0)
            attention_tensor(pe)
            ffn_tensor(pe, ffn[1], 1)

        @block.scalar
        def _(act):
            ffn_scalar(act, ffn[0], 0)
            attention_scalar(act)
            ffn_scalar(act, ffn[1], 1)

        @block.vector
        def _(dve):
            dve.memset(blank[:, :], 0.0).then_inc(const_set, 1)
            dve.wait_ge(con_in, 16)
            dve.tensor_copy(XN[:, PT:TILES, D], con[:, C_TOKEN:C_TOKEN + PT]).then_inc(const_set, 1)
            dve.memset(ones[:, :], 1.0).then_inc(const_set, 1)
            ffn_vector(dve, ffn[0], 0)
            attention_vector(dve)
            ffn_vector(dve, ffn[1], 1)
            for t in range(PT, TILES):
                if t % ROW == 0:
                    dve.wait_ge(ffn[1].gathered[t // ROW], 16)
                add_back(dve, ffn[1], t)

        @block.gpsimd
        def _(pool):
            ffn_gpsimd(pool, ffn[0], 0)
            attention_gpsimd(pool)
            ffn_gpsimd(pool, ffn[1], 1)


def even_odd(w):
    return w.reshape(D, HEADS, HEAD // 2, 2).transpose(0, 1, 3, 2).reshape(D, HEADS * HEAD)


def kernel(L0_attn_x, L0_attn_Wq, L0_attn_Wk, L0_attn_Wv, L0_attn_Wo, L0_ffn_Wr, L0_ffn_br, L0_ffn_W1, L0_ffn_b1,
           L0_ffn_W2, L0_ffn_b2):
    import numpy as np
    import concourse.bacc as bacc
    from concourse.bass_utils import run_bass_kernel_spmd

    arrays = {
        "x": np.asarray(L0_attn_x), "wq": even_odd(np.asarray(L0_attn_Wq)), "wk": even_odd(np.asarray(L0_attn_Wk)),
        "wv": np.asarray(L0_attn_Wv), "wo": np.asarray(L0_attn_Wo), "wr": np.asarray(L0_ffn_Wr),
        "br": np.asarray(L0_ffn_br), "w1": np.asarray(L0_ffn_W1), "b1": np.asarray(L0_ffn_b1),
        "w2": np.asarray(L0_ffn_W2), "b2": np.asarray(L0_ffn_b2), "consts": constants(),
    }
    arrays = {f"in_{name}": np.ascontiguousarray(a) for name, a in arrays.items()}
    nc = bacc.Bacc("TRN2", target_bir_lowering=False, num_devices=1)
    args = [nc.dram_tensor(name, a.shape, mybir.dt.from_np(a.dtype), kind="ExternalInput").ap()
            for name, a in arrays.items()]
    out = nc.dram_tensor("out_0", (BATCH, SEQ, D), F32, kind="ExternalOutput").ap()
    macaron_kernel(nc, *args, out)
    r = run_bass_kernel_spmd(nc, [arrays], core_ids=[0])
    return r.results[0]["out_0"]
```
